# Optimizing a Trainium2 kernel written in Bass

```python
import numpy as np
import jax
import jax.numpy as jnp

def _softmax(x, axis=-1):
    return jax.nn.softmax(x, axis=axis)

def _gelu(x):
    return jax.nn.gelu(x, approximate=True)

def _silu(x):
    return jax.nn.silu(x)

def _sigmoid(x):
    return jax.nn.sigmoid(x)

def _layernorm(x, axis=-1, eps=1e-05):
    m = jnp.mean(x, axis=axis, keepdims=True)
    v = jnp.var(x, axis=axis, keepdims=True)
    return (x - m) / jnp.sqrt(v + eps)

def _scatter_add(tgt, idx, src, axis=0):
    return tgt.at[idx].add(src)

def _segment_sum(src, seg, n):
    return jax.ops.segment_sum(src, seg, n)
kernel_name = 'mk_macaron_d1_jaxref_r8_d86179'

def setup_inputs(seed: int=0):
    np.random.seed(seed)
    _w = jnp.asarray

    def _L0_attn_setup():
        import jax, jax.numpy as jnp
        import numpy as np
        import math
        D_MODEL, D_C, D_R, NH = (128, 128, 32, 16)
        HD = D_MODEL // NH
        B, T = (2, 256)

        def _rope_tables(T, d_R):
            inv_freq = 1.0 / 10000.0 ** (jnp.arange(0, d_R, 2, dtype=jnp.float32) / d_R)
            t = jnp.arange(T, dtype=jnp.float32)
            freqs = jnp.outer(t, inv_freq)
            return (jnp.cos(freqs), jnp.sin(freqs))

        def _rotary_apply(x, cos, sin):
            d = x.shape[-1]
            x1, x2 = (x[..., :d // 2], x[..., d // 2:])
            return jnp.concatenate([x1 * cos - x2 * sin, x2 * cos + x1 * sin], axis=-1)
        key = jax.random.key(seed)
        ks = jax.random.split(key, 8)
        s = lambda fan_in: 1.0 / math.sqrt(fan_in)
        return {'x': jax.random.normal(ks[0], (B, T, D_MODEL), jnp.float32), 'W_kv_down': jax.random.normal(ks[1], (D_MODEL, D_C), jnp.float32) * s(D_MODEL), 'W_k_up': jax.random.normal(ks[2], (D_C, D_MODEL), jnp.float32) * s(D_C), 'W_v_up': jax.random.normal(ks[3], (D_C, D_MODEL), jnp.float32) * s(D_C), 'W_q': jax.random.normal(ks[4], (D_MODEL, D_MODEL), jnp.float32) * s(D_MODEL), 'W_q_rope': jax.random.normal(ks[5], (D_MODEL, D_R), jnp.float32) * s(D_MODEL), 'W_k_rope': jax.random.normal(ks[6], (D_C, D_R), jnp.float32) * s(D_C), 'W_o': jax.random.normal(ks[7], (D_MODEL, D_MODEL), jnp.float32) * s(D_MODEL)}
    _L0_attn_in = _L0_attn_setup()

    def _L0_ffn_setup():
        import jax, jax.numpy as jnp
        import numpy as np
        TOP_K = 8
        NUM_EXPERTS = 32
        CAPACITY = 128
        key = jax.random.key(seed)
        k1, k2, k3, k4 = jax.random.split(key, 4)
        B, S, H, E, F = (2, 128, 128, NUM_EXPERTS, 96)
        return {'hidden_states': jax.random.normal(k1, (B, S, H), dtype=jnp.float32), 'gate_weight': jax.random.normal(k2, (E, H), dtype=jnp.float32) * 0.02, 'gate_up_proj': jax.random.normal(k3, (E, 2 * F, H), dtype=jnp.float32) * 0.02, 'down_proj': jax.random.normal(k4, (E, H, F), dtype=jnp.float32) * 0.02}
    _L0_ffn_in = _L0_ffn_setup()
    _d = {'L0_attn_x': _L0_attn_in['x'], 'L0_attn_W_kv_down': _L0_attn_in['W_kv_down'], 'L0_attn_W_k_up': _L0_attn_in['W_k_up'], 'L0_attn_W_v_up': _L0_attn_in['W_v_up'], 'L0_attn_W_q': _L0_attn_in['W_q'], 'L0_attn_W_q_rope': _L0_attn_in['W_q_rope'], 'L0_attn_W_k_rope': _L0_attn_in['W_k_rope'], 'L0_attn_W_o': _L0_attn_in['W_o'], 'L0_ffn_gate_weight': _L0_ffn_in['gate_weight'], 'L0_ffn_gate_up_proj': _L0_ffn_in['gate_up_proj'], 'L0_ffn_down_proj': _L0_ffn_in['down_proj']}
    _x0 = _d['L0_attn_x']
    _d['L0_attn_x'] = jax.random.normal(jax.random.fold_in(jax.random.key(seed), 1), (2, 1024, 128), dtype=_x0.dtype)
    del _x0
    return _d

def reference(L0_attn_x, L0_attn_W_kv_down, L0_attn_W_k_up, L0_attn_W_v_up, L0_attn_W_q, L0_attn_W_q_rope, L0_attn_W_k_rope, L0_attn_W_o, L0_ffn_gate_weight, L0_ffn_gate_up_proj, L0_ffn_down_proj):

    def _L0_attn_ref(x, W_kv_down, W_k_up, W_v_up, W_q, W_q_rope, W_k_rope, W_o):
        import jax, jax.numpy as jnp
        import numpy as np
        import math
        D_MODEL, D_C, D_R, NH = (128, 128, 32, 16)
        HD = D_MODEL // NH
        B, T = (2, 256)

        def _rope_tables(T, d_R):
            inv_freq = 1.0 / 10000.0 ** (jnp.arange(0, d_R, 2, dtype=jnp.float32) / d_R)
            t = jnp.arange(T, dtype=jnp.float32)
            freqs = jnp.outer(t, inv_freq)
            return (jnp.cos(freqs), jnp.sin(freqs))

        def _rotary_apply(x, cos, sin):
            d = x.shape[-1]
            x1, x2 = (x[..., :d // 2], x[..., d // 2:])
            return jnp.concatenate([x1 * cos - x2 * sin, x2 * cos + x1 * sin], axis=-1)
        Bb, Tt, _ = x.shape
        cos, sin = _rope_tables(Tt, D_R)
        cos = cos[None]
        sin = sin[None]
        c_kv = x @ W_kv_down
        k_rope = _rotary_apply(c_kv @ W_k_rope, cos, sin)
        k = (c_kv @ W_k_up).reshape(Bb, Tt, NH, HD)
        v = (c_kv @ W_v_up).reshape(Bb, Tt, NH, HD)
        q = (x @ W_q).reshape(Bb, Tt, NH, HD)
        q_rope = _rotary_apply(x @ W_q_rope, cos, sin)
        scale = math.sqrt(HD + D_R)
        scores = jnp.einsum('bqhd,bkhd->bhqk', q, k)
        scores = scores + jnp.einsum('bqr,bkr->bqk', q_rope, k_rope)[:, None]
        scores = scores / scale
        causal = jnp.triu(jnp.ones((Tt, Tt), dtype=bool), k=1)
        scores = jnp.where(causal[None, None], -jnp.inf, scores)
        w = jax.nn.softmax(scores, axis=-1)
        attn = jnp.einsum('bhqk,bkhd->bqhd', w, v).reshape(Bb, Tt, D_MODEL)
        return attn @ W_o

    def _L0_ffn_ref(hidden_states, gate_weight, gate_up_proj, down_proj):
        import jax, jax.numpy as jnp
        import numpy as np
        TOP_K = 8
        NUM_EXPERTS = 32
        CAPACITY = 128
        B, S, H = hidden_states.shape
        E = gate_weight.shape[0]
        N = B * S
        x = hidden_states.reshape(N, H)
        logits = x @ gate_weight.T
        probs = jax.nn.softmax(logits.astype(jnp.float32), axis=-1)
        topw, topi = jax.lax.top_k(probs, TOP_K)
        topw = topw / topw.sum(-1, keepdims=True)
        topw = topw.astype(x.dtype)
        flat_e = topi.reshape(-1)
        flat_w = topw.reshape(-1)
        flat_x = jnp.repeat(x, TOP_K, axis=0)
        oh = jax.nn.one_hot(flat_e, E, dtype=jnp.int32)
        pos = (jnp.cumsum(oh, axis=0) * oh).sum(-1) - 1
        buf = jnp.zeros((E, CAPACITY, H), x.dtype).at[flat_e, pos].set(flat_x, mode='drop')
        gu = jnp.einsum('ech,efh->ecf', buf, gate_up_proj)
        gate, up = jnp.split(gu, 2, axis=-1)
        h = jax.nn.silu(gate) * up
        eo = jnp.einsum('ecf,ehf->ech', h, down_proj)
        tok_out = eo.at[flat_e, pos].get(mode='fill', fill_value=0)
        out = (tok_out * flat_w[:, None]).reshape(N, TOP_K, H).sum(1)
        return out.reshape(B, S, H)
    x = L0_attn_x
    x = x + 0.5 * _L0_ffn_ref(_layernorm(x, axis=-1), L0_ffn_gate_weight, L0_ffn_gate_up_proj, L0_ffn_down_proj)
    x = x + _L0_attn_ref(_layernorm(x, axis=-1), L0_attn_W_kv_down, L0_attn_W_k_up, L0_attn_W_v_up, L0_attn_W_q, L0_attn_W_q_rope, L0_attn_W_k_rope, L0_attn_W_o)
    x = x + 0.5 * _L0_ffn_ref(_layernorm(x, axis=-1), L0_ffn_gate_weight, L0_ffn_gate_up_proj, L0_ffn_down_proj)
    return x

_drawn_inputs = setup_inputs


def setup_inputs(seed=0):
    import zlib

    import numpy as np

    out = dict(_drawn_inputs(seed))
    spreads = {}
    factors = {'L0_ffn_gate_weight': 8.0, 'L0_ffn_gate_up_proj': 8.0, 'L0_ffn_down_proj': 8.0}
    for name, (base, spread) in spreads.items():
        noise = np.random.default_rng([zlib.crc32(name.encode()), seed]).standard_normal(out[name].shape)
        drawn = base * np.exp(spread * noise) if base else spread * noise
        out[name] = jnp.asarray(drawn.astype(out[name].dtype))
    for name, factor in factors.items():
        out[name] = (out[name] * factor).astype(out[name].dtype)
    return out
```

```python
from contextlib import ExitStack

import numpy as np
import concourse.bass as bass
from concourse import mybir

F32 = mybir.dt.float32
F32R = mybir.dt.float32r
BF16 = mybir.dt.bfloat16
ALU = mybir.AluOpType
ACT = mybir.ActivationFunctionType
AX = mybir.AxisListType

P = 128
B, T, D = 2, 1024, 128
N = B * T
NT = N // P
TB = T // P
NH, HD, DR = 16, 8, 32
E, F, TOPK, CAP = 32, 96, 8, 128
CE = 4
NCH = E // CE
BANK = 512
NPAIR = NH // 2
ROPE3 = 3 * DR
NOPE3 = 3 * HD
ROWS = ROPE3 + NOPE3
VW = 32
SCALE = 1.0 / float(np.sqrt(HD + DR))
EPS = 1e-5
UNROUTED = 4096.0
MASKED = -1e30
RING = 2

STEPS = [(j, i) for j in range(T // BANK) for i in range((j + 1) * BANK // P)]
NS = len(STEPS)


def build(nc, x_in, w_kv_down, w_k_up, w_v_up, w_q, w_q_rope, w_k_rope, w_o,
          gate_weight, gate_up_proj, down_proj, squares, cos3, sin3, iota, tokinfo, out):
    ctx = ExitStack()

    def sb(name, shape, dt=F32, stack=None):
        return (stack or ctx).enter_context(nc.sbuf_tensor(name, shape, dt))

    def sem(name):
        return ctx.enter_context(nc.semaphore(name))

    def dram(name, shape, dt):
        return nc.dram_tensor(name, shape, dt).ap()

    with ctx:
        guT_d = dram("guT_d", [NCH, P, CE * 2 * F], F32)
        dnT_d = dram("dnT_d", [NCH, F, CE * D], F32)
        kn_d = dram("kn_d", [3, NH * HD, N], F32)
        qn_d = dram("qn_d", [3, NH * HD, N], F32)
        shift_d = dram("shift_d", [NH, N], F32)

        x = sb("x", [P, NT, D])
        sq = sb("sq", [P, 4, P])
        ident = sq[:, 0, :]
        identb = sb("identb", [P, P], BF16)
        tri = sb("tri", [P, P], BF16)
        maskT = sb("maskT", [P, P], BF16)
        maskQ = sb("maskQ", [P, P], BF16)
        onesb = sb("onesb", [P, P], BF16)
        zerosb = sb("zerosb", [P, BANK], BF16)
        gate_n = sb("gate_n", [E, D])
        gateT = sb("gateT", [D, E])
        iota_s = sb("iota_s", [P, N])
        iotab = sb("iotab", [P, P], BF16)
        tokinfo_s = sb("tokinfo_s", [P, NT, 2])
        stats = sb("stats", [P, NT, 6])
        mv = sb("mv", [P, NT, 2])
        var = sb("var", [P, NT])
        sd = sb("sd", [P, NT])
        rstd = sb("rstd", [P, NT])
        xs = [sb(f"xs{p}", [P, D]) for p in range(RING)]
        gus = [sb(f"gus{p}", [P, CE, 2, F]) for p in range(RING)]
        dns = [sb(f"dns{p}", [F, CE, D]) for p in range(RING)]
        eoh = [sb(f"eoh{p}", [P, CE, D], F32R) for p in range(RING)]
        eol = [sb(f"eol{p}", [P, CE, D], F32R) for p in range(RING)]
        Q1 = [sb(f"Q1{p}", [P, N], F32R) for p in range(RING)]

        moe = ExitStack()
        wgn = [sb(f"wgn{p}", [F, CE * 2, D], F32, moe) for p in range(RING)]
        wdn = [sb(f"wdn{p}", [D, CE, F], F32, moe) for p in range(RING)]
        xt = [sb(f"xt{p}", [D, P], F32, moe) for p in range(RING)]
        xp = sb("xp", [P, NT, 3, D], BF16, moe)
        rem = sb("rem", [P, D], F32, moe)
        rem2 = sb("rem2", [P, D], F32, moe)
        negmax = sb("negmax", [P, NT], F32, moe)
        zl = sb("zl", [P, NT, E], F32, moe)
        pr = sb("pr", [P, NT, E], F32, moe)
        den = sb("den", [P, NT], F32, moe)
        rden = sb("rden", [P, NT], F32, moe)
        t8 = sb("t8", [P, NT, TOPK], F32, moe)
        rep = sb("rep", [P, NT, E], F32, moe)
        maskb = sb("maskb", [P, NT, E], BF16, moe)
        wr = sb("wr", [P, NT, E], F32, moe)
        info = sb("info", [P, NT, E, 5], BF16, moe)
        posm = sb("posm", [P, NT, E], F32, moe)
        onehot = sb("onehot", [P, NT, CE, CAP], BF16, moe)
        bufT = [sb(f"bufT{p}", [D, CE, CAP], F32, moe) for p in range(RING)]
        idx = sb("idx", [P, CE, 8], F32, moe)
        tok = sb("tok", [P, CE], F32, moe)
        wslot = [sb(f"wslot{p}", [P, CE], F32, moe) for p in range(RING)]
        wtmp = sb("wtmp", [P, CE], F32, moe)
        th = sb("th", [F, CE, CAP], F32, moe)
        ga = sb("ga", [F, CE, CAP], F32, moe)
        hT = sb("hT", [F, CE, CAP], F32, moe)
        yT = sb("yT", [D, N], F32, moe)
        moe.close()

        att = ExitStack()
        xnT = sb("xnT", [D, N], F32, att)
        ckvT = sb("ckvT", [D, N], F32, att)
        wat = sb("wat", [P, 5, D], F32, att)
        wrope = sb("wrope", [P, 2, DR], F32, att)
        wrep = sb("wrep", [P, 2, 2, 3, DR], F32, att)
        cs = sb("cs", [ROPE3, 2, T], F32, att)
        ra = sb("ra", [ROPE3, BANK], F32, att)
        rb = sb("rb", [ROPE3, BANK], F32, att)
        nh = [sb(f"nh{p}", [P, BANK], F32R, att) for p in range(RING)]
        nl = [sb(f"nl{p}", [P, BANK], F32R, att) for p in range(RING)]
        V = sb("V", [P, NT, NH, HD], F32, att)
        Vst = [sb(f"Vst{p}", [P, NT, 2, VW], F32, att) for p in range(RING)]
        Kst = [[sb(f"Kst{p}{h}", [P, N], F32R, att) for h in range(2)] for p in range(RING)]
        Qst = [[sb(f"Qst{p}{h}", [P, N], F32R, att) for h in range(2)] for p in range(RING)]
        probs = [sb(f"probs{p}", [P, 4, BANK], F32, att) for p in range(RING)]
        mx = sb("mx", [P, 2 * NT], F32, att)
        shf = sb("shf", [2 * NT, P], F32R, att)
        oS = [sb(f"oS{j}", [P, BANK], F32, att) for j in range(2)]
        ord_ = sb("ord", [P, 4, 4], F32, att)
        attn = sb("attn", [P, NT, D], F32, att)
        attnT = [sb(f"attnT{p}", [D, P], F32, att) for p in range(RING)]
        att.close()

        ps = ctx.enter_context(nc.psum_tensor("ps", [P, 8, BANK], F32))

        gc_s = sem("gc_s")
        var_s = sem("var_s")
        sd_s = sem("sd_s")
        consts_in = sem("consts_in")
        x_in_s = sem("x_in_s")
        gate_in = sem("gate_in")
        watt_in = sem("watt_in")
        consts_b = sem("consts_b")
        zeros_b = sem("zeros_b")
        tok_b = sem("tok_b")
        gate_t = sem("gate_t")
        gate_c = sem("gate_c")
        w_nat = [sem(f"w_nat{p}") for p in range(RING)]
        w_tr = sem("w_tr")
        w_c1 = sem("w_c1")
        w_c2 = sem("w_c2")
        w_store = sem("w_store")
        st_s = sem("st_s")
        mv_s = sem("mv_s")
        rstd_s = sem("rstd_s")
        xs_s = sem("xs_s")
        tr_s = sem("tr_s")
        xt_s = sem("xt_s")
        lg_s = sem("lg_s")
        xp_s = sem("xp_s")
        rem_s1 = sem("rem_s1")
        rem_s2 = sem("rem_s2")
        r_s = sem("r_s")
        ez_s = sem("ez_s")
        pos_s = sem("pos_s")
        tmax = sem("tmax")
        trep = sem("trep")
        posm_s = sem("posm_s")
        r2_s = sem("r2_s")
        oh_s = sem("oh_s")
        ga_s = sem("ga_s")
        bufT_s = sem("bufT_s")
        idx_s = sem("idx_s")
        tok_c = sem("tok_c")
        ws_s = sem("ws_s")
        gus_in = [sem(f"gus_in{p}") for p in range(RING)]
        dns_in = [sem(f"dns_in{p}") for p in range(RING)]
        gu_s = sem("gu_s")
        th_s = sem("th_s")
        sl_s = sem("sl_s")
        eo_s = sem("eo_s")
        eoh_s = sem("eoh_s")
        eol_s = sem("eol_s")
        q1_s = sem("q1_s")
        q1_free = sem("q1_free")
        y_s = sem("y_s")
        yT_s = sem("yT_s")
        yt_s = sem("yt_s")
        xa_s = sem("xa_s")
        wrep_s = sem("wrep_s")
        ckv_s = sem("ckv_s")
        ckv_c = sem("ckv_c")
        np_s = sem("np_s")
        nh_s = sem("nh_s")
        nl_s = sem("nl_s")
        nh_st = [sem(f"nh_st{p}") for p in range(RING)]
        rp_s = sem("rp_s")
        rp_a = sem("rp_a")
        rp_b = sem("rp_b")
        rp_h = sem("rp_h")
        rp_l = sem("rp_l")
        ropek = sem("ropek")
        v_s = sem("v_s")
        v_c = sem("v_c")
        vst_s = sem("vst_s")
        vst_z = sem("vst_z")
        kst_in = [sem(f"kst_in{p}") for p in range(RING)]
        ones_s = sem("ones_s")
        mS_s = sem("mS_s")
        mx_s = sem("mx_s")
        mxt_s = sem("mxt_s")
        shf_s = sem("shf_s")
        shf_st = sem("shf_st")
        st_ready = sem("st_ready")
        pr_s = sem("pr_s")
        pr_free = sem("pr_free")
        oS_s = sem("oS_s")
        ot_s = sem("ot_s")
        or_s = sem("or_s")
        om_s = sem("om_s")
        at_s = sem("at_s")
        at_c = sem("at_c")
        wo_s = sem("wo_s")
        out_s = sem("out_s")

        blk = ctx.enter_context(nc.Block())

        def flat(a):
            return a.rearrange("p a b -> p (a b)")

        def raw(a):
            return a.bitcast(F32)

        @blk.sync
        def _(e):
            e.dma_start(sq[:, :, :], squares.rearrange("k p c -> p k c")).then_inc(consts_in, 16)
            e.dma_start(tokinfo_s[:, :, :], tokinfo).then_inc(consts_in, 16)
            e.dma_start(iota_s[:, :], iota.broadcast_to([P, N])).then_inc(consts_in, 16)
            e.dma_start(gate_n[:, :], gate_weight).then_inc(gate_in, 16)
            e.dma_start(x[:, :, :], x_in.rearrange("b (t p) d -> p (b t) d", p=P)).then_inc(x_in_s, 16)
            with e.Fori(0, NCH // RING) as i:
                for p in range(RING):
                    c = i * RING + p
                    e.wait_ge(w_tr, c + 1)
                    e.dma_start(wgn[p][:, :, :], gate_up_proj[bass.ds(c * CE, CE)].rearrange("e (s f) h -> f (e s) h", s=2)).then_inc(w_nat[p], 16)
                    e.dma_start(wdn[p][:, :, :], down_proj[bass.ds(c * CE, CE)].rearrange("e h f -> h e f")).then_inc(w_nat[p], 16)
                    e.wait_ge(w_c1, c + 2)
                    e.wait_ge(w_c2, c + 2)
                    e.dma_start(guT_d[bass.ds(c, 1)].rearrange("o p n -> (o p) n"), gus[p][:, :, :, :].rearrange("p a b c -> p (a b c)")).then_inc(w_store, 16)
                    e.dma_start(dnT_d[bass.ds(c, 1)].rearrange("o p n -> (o p) n"), flat(dns[p][:, :, :])).then_inc(w_store, 16)
            e.wait_ge(w_store, 32 * NCH)

            def stage_weights(k):
                with e.Fori(0, NCH // RING) as i:
                    for p in range(RING):
                        c = k * NCH + i * RING + p
                        e.wait_ge(eo_s, c + 1)
                        e.dma_start(gus[p][:, :, :, :].rearrange("p a b c -> p (a b c)"), guT_d[bass.ds(i * RING + p, 1)].rearrange("o p n -> (o p) n")).then_inc(gus_in[p], 16)
                        e.dma_start(flat(dns[p][:, :, :]), dnT_d[bass.ds(i * RING + p, 1)].rearrange("o p n -> (o p) n")).then_inc(dns_in[p], 16)

            stage_weights(0)
            e.wait_ge(xa_s, NT + RING)
            for n, w in enumerate((w_kv_down, w_k_up, w_v_up, w_q, w_o)):
                e.dma_start(wat[:, n, :], w).then_inc(watt_in, 16)
            e.dma_start(wrope[:, 0, :], w_k_rope).then_inc(watt_in, 16)
            e.dma_start(wrope[:, 1, :], w_q_rope).then_inc(watt_in, 16)
            e.dma_start(cs[:, 0, :], cos3).then_inc(watt_in, 16)
            e.dma_start(cs[:, 1, :], sin3).then_inc(watt_in, 16)
            for side, (dst, parts) in enumerate(((kn_d, "hlh"), (qn_d, "hhl"))):
                for c in range(N // BANK):
                    u = side * (N // BANK) + c
                    e.wait_ge(nh_s, u + 1)
                    e.wait_ge(nl_s, u + 1)
                    for r, part in enumerate(parts):
                        src = nh[u % RING] if part == "h" else nl[u % RING]
                        e.dma_start(dst[r, :, c * BANK:(c + 1) * BANK], raw(src[:, :])).then_inc(nh_st[u % RING], 16)
            e.wait_ge(rp_l, 2 * N // BANK)
            e.wait_ge(rp_h, 2 * N // BANK)
            e.wait_ge(ones_s, 8)
            for st in (Kst, Qst):
                for p, h in ((0, 1), (1, 0), (1, 1)):
                    e.dma_start(raw(st[p][h][0:ROPE3, :]), raw(st[0][0][0:ROPE3, :])).then_inc(ropek, 16)
            for q in range(RING):
                e.wait_ge(nh_st[q], 48 * N // BANK)

            def stage_heads(phase):
                with e.Fori(0, NPAIR // RING) as i:
                    for p in range(RING):
                        pair = i * RING + p
                        e.wait_ge(st_ready, 2 * NS * (pair + 1))
                        for h in range(2):
                            rows = bass.ds((pair * 2 + h) * HD, HD)
                            e.dma_start(raw(Kst[p][h][ROPE3:ROWS, :]), kn_d[:, rows, :]).then_inc(kst_in[p], 16)
                            e.dma_start(raw(Qst[p][h][ROPE3:ROWS, :]), qn_d[:, rows, :]).then_inc(kst_in[p], 16)
                            if phase == 1:
                                e.dma_start(raw(Qst[p][h][ROWS:ROWS + 1, :]), shift_d[bass.ds(pair * 2 + h, 1), :]).then_inc(kst_in[p], 16)

            with e.Fori(0, NPAIR // RING) as i:
                for p in range(RING):
                    pair = i * RING + p
                    e.wait_ge(mS_s, 4 * TB * (pair + 1))
                    for h in range(2):
                        rows = bass.ds((pair * 2 + h) * HD, HD)
                        e.dma_start(raw(Kst[p][h][ROPE3:ROWS, :]), kn_d[:, rows, :]).then_inc(kst_in[p], 16)
                        e.dma_start(raw(Qst[p][h][ROPE3:ROWS, :]), qn_d[:, rows, :]).then_inc(kst_in[p], 16)
                    e.wait_ge(shf_s, pair + 2)
                    e.dma_start(shift_d[bass.ds(pair * 2, 2), :].rearrange("h (t q) -> (h t) q", q=P), raw(shf[:, :])).then_inc(shf_st, 16)
            e.wait_ge(shf_st, 16 * (NPAIR + 1))
            stage_heads(1)
            e.wait_ge(xa_s, 2 * NT + RING)
            stage_weights(1)
            e.wait_ge(xa_s, 3 * NT + RING)
            e.dma_start(out.rearrange("b (t p) d -> p (b t) d", p=P), x[:, :, :]).then_inc(out_s, 16)
            e.wait_ge(out_s, 16)

        @blk.gpsimd
        def _(e):
            e.memset(onesb[:, :], 1.0).then_inc(zeros_b, 1)
            e.memset(zerosb[:, :], 0.0).then_inc(zeros_b, 1)
            e.wait_ge(consts_in, 48)
            e.tensor_copy(identb[:, :], sq[:, 0, :]).then_inc(consts_b, 1)
            e.tensor_copy(tri[:, :], sq[:, 1, :]).then_inc(consts_b, 1)
            e.tensor_copy(maskT[:, :], sq[:, 2, :]).then_inc(consts_b, 1)
            e.tensor_copy(maskQ[:, :], sq[:, 3, :]).then_inc(consts_b, 1)
            e.tensor_copy(iotab[:, :], iota_s[:, 0:P]).then_inc(consts_b, 1)

            def split(k):
                for q in range(2):
                    e.tensor_copy(info[:, :, :, q], tokinfo_s[:, :, q:q + 1].broadcast_to([P, NT, E])).then_inc(tok_b, 1)
                for t in range(NT):
                    p = t % RING
                    u = k * NT + t
                    e.wait_ge(xs_s, 2 * k * NT + t + 1)
                    part = lambda q: xp[:, t, q, :]
                    e.tensor_copy(part(0), xs[p][:, :]).then_inc(rem_s1, 1)
                    e.wait_ge(rem_s1, 2 * (u + RING) + 1)
                    e.tensor_tensor(rem[:, :], xs[p][:, :], part(0), ALU.subtract).then_inc(rem_s1, 1)
                    e.wait_ge(rem_s1, 2 * (u + RING) + 2)
                    e.tensor_copy(part(1), rem[:, :]).then_inc(rem_s2, 1)
                    e.wait_ge(rem_s2, 2 * u + 1)
                    e.tensor_tensor(rem2[:, :], rem[:, :], part(1), ALU.subtract).then_inc(rem_s2, 1)
                    e.wait_ge(rem_s2, 2 * u + 2)
                    e.tensor_copy(part(2), rem2[:, :]).then_inc(xp_s, 1)

            e.sem_inc(w_c1, 1)
            e.sem_inc(w_c2, 1)
            e.sem_inc(idx_s, 1)
            e.sem_inc(eol_s, 1)
            e.sem_inc(bufT_s, 1)
            e.sem_inc(sl_s, 1)
            e.sem_inc(mxt_s, 1)
            e.sem_inc(om_s, 1)
            e.sem_inc(shf_s, 1)
            e.sem_inc(shf_st, 16)
            e.sem_inc(rem_s1, 2 * RING)
            split(0)
            e.wait_ge(xa_s, NT + RING)
            for p in range(RING):
                for h in range(2):
                    e.memset(raw(Kst[p][h][ROPE3:P, :]), 1.0).then_inc(ones_s, 1)
                    e.memset(raw(Qst[p][h][ROPE3:P, :]), 0.0).then_inc(ones_s, 1)
            e.wait_ge(ones_s, 8)
            for p in range(RING):
                e.memset(Vst[p][:, :, :, HD:VW], 0.0).then_inc(vst_z, 1)
            e.wait_ge(vst_z, RING)
            for p in range(RING):
                e.memset(Vst[p][:, :, :, HD:HD + 1], 1.0).then_inc(vst_z, 1)
            e.wait_ge(watt_in, 16 * 9)
            for side in range(2):
                e.tensor_copy(wrep[:, side, 0, :, :], wrope[:, side:side + 1, :].broadcast_to([P, 3, DR])).then_inc(wrep_s, 1)
                half = DR // 2
                e.tensor_copy(wrep[:, side, 1, :, 0:half], wrope[:, side:side + 1, half:DR].broadcast_to([P, 3, half])).then_inc(wrep_s, 1)
                e.tensor_copy(wrep[:, side, 1, :, half:DR], wrope[:, side:side + 1, 0:half].broadcast_to([P, 3, half])).then_inc(wrep_s, 1)
            e.wait_ge(v_c, 4)
            with e.Fori(0, NPAIR // RING) as i:
                for p in range(RING):
                    pair = i * RING + p
                    e.wait_ge(pr_free, NS * (pair + 1))
                    e.tensor_copy(Vst[p][:, :, :, 0:HD], V[:, :, bass.ds(pair * 2, 2), :]).then_inc(vst_s, 1)
            split(1)

        @blk.scalar
        def _(e):
            e.wait_ge(gate_t, 1)
            e.activation(gateT[:, :], ps[:, 2, 0:E], ACT.Copy).then_inc(gate_c, 1)
            e.sem_inc(eo_s, RING)
            with e.Fori(0, NCH // RING) as i:
                for p in range(RING):
                    c = i * RING + p
                    e.wait_ge(w_tr, c + 1 + RING)
                    e.activation(gus[p][:, :, :, :].rearrange("p (g e) s f -> p g (e s f)", g=2), ps[:, 3:5, 0:CE * F], ACT.Copy).then_inc(w_c1, 1)

            def transposed(n):
                e.wait_ge(var_s, n + 1)
                e.activation(sd[:, :], var[:, :], ACT.Sqrt).then_inc(sd_s, 1)
                with e.Fori(0, NT // RING) as i:
                    for p in range(RING):
                        t = i * RING + p
                        u = n * NT + t
                        e.wait_ge(tr_s, u + 1 + RING)
                        if n == 1:
                            e.activation(xnT[:, bass.ds(t * P, P)], ps[:, p, 0:P], ACT.Copy).then_inc(xt_s, 1)
                        else:
                            e.wait_ge(lg_s, (n // 2) * NT + t + 1)
                            e.activation(xt[p][:, :], ps[:, p, 0:P], ACT.Copy).then_inc(xt_s, 1)

            def experts(k):
                e.wait_ge(r_s, 2 + 5 * k)
                e.activation(zl[:, :, :], zl[:, :, :], ACT.Exp).then_inc(ez_s, 1)
                with e.Fori(0, NCH // RING) as i:
                    for p in range(RING):
                        c = k * NCH + i * RING + p
                        e.wait_ge(gc_s, c + 1)
                        e.wait_ge(gu_s, c + 1)
                        e.activation(flat(bufT[p][:, :, :]), ps[:, 0, :], ACT.Copy).then_inc(bufT_s, 1)
                        e.wait_ge(gu_s, c + 1 + RING)
                        e.wait_ge(sl_s, 2 * c + 1)
                        e.activation(flat(th[:, :, :]), ps[0:F, 1, :], ACT.Tanh, scale=0.5).then_inc(th_s, 1)
                        e.wait_ge(eo_s, c + 1 + RING)
                        e.wait_ge(ws_s, c + 1)
                        e.wait_ge(q1_free, CE * (c + 1))
                        for q in range(CE):
                            last = e.activation(eoh[p][:, q, :], ps[:, 1, q * D:(q + 1) * D], ACT.Copy, scale=wslot[p][:, q:q + 1])
                        last.then_inc(eoh_s, 1)
                e.wait_ge(y_s, k + 1)
                e.activation(yT[:, :].rearrange("p (a b) -> p a b", a=4), ps[:, 4:8, :], ACT.Copy).then_inc(yT_s, 1)

            e.sem_inc(xt_s, RING)
            transposed(0)
            experts(0)
            transposed(1)
            for c in range(N // BANK):
                e.wait_ge(ckv_s, c + 1)
                e.activation(ckvT[:, c * BANK:(c + 1) * BANK], ps[:, c % 2, :], ACT.Copy).then_inc(ckv_c, 1)
            with e.Fori(0, NPAIR // RING) as i:
                for p in range(RING):
                    pair = i * RING + p
                    e.wait_ge(mxt_s, pair + 2)
                    e.wait_ge(shf_st, 16 * (pair + 1))
                    e.activation(shf[:, :], ps[0:2 * NT, 6, 0:P], ACT.Copy, scale=-1.0).then_inc(shf_s, 1)
            with e.Fori(0, NPAIR // RING) as i:
                for p in range(RING):
                    pair = i * RING + p
                    for n, (j, kt) in enumerate(STEPS):
                        lo = max(0, kt * P - j * BANK)
                        for b in range(B):
                            e.wait_ge(st_ready, (pair + 2) * 2 * NS + 2 * n + b + 1)
                            if b == 0:
                                e.wait_ge(pr_free, (pair + 2) * NS + n + 1 - RING)
                            e.activation(probs[n % RING][:, 2 * b:2 * b + 2, lo:BANK], ps[:, 2 * b:2 * b + 2, lo:BANK],
                                         ACT.Exp, scale=SCALE).then_inc(pr_s, 1)
            for t in range(NT):
                e.wait_ge(at_s, t + 1)
                e.wait_ge(wo_s, t + 1)
                e.activation(attnT[t % RING][:, :], ps[:, t % 2, 0:P], ACT.Copy).then_inc(at_c, 1)
            transposed(2)
            experts(1)

        @blk.vector
        def _(e):
            with e.Fori(0, NCH // RING) as i:
                for p in range(RING):
                    c = i * RING + p
                    e.wait_ge(w_tr, c + 1 + RING)
                    e.tensor_copy(flat(dns[p][:, :, :]), ps[0:F, 5, :]).then_inc(w_c2, 1)

            def layernorm(n):
                with e.Fori(0, NT) as t:
                    e.bn_stats(flat(stats[:, bass.ds(t, 1), :]), flat(x[:, bass.ds(t, 1), :])).then_inc(st_s, 1)
                e.wait_ge(st_s, NT * (n + 1))
                for t in range(NT):
                    e.bn_aggr(mv[:, t, :], stats[:, t, :]).then_inc(mv_s, 1)
                e.wait_ge(mv_s, NT * (n + 1))
                e.tensor_scalar(var[:, :], mv[:, :, 1], EPS, None, ALU.add).then_inc(var_s, 1)
                e.wait_ge(sd_s, n + 1)
                e.reciprocal(rstd[:, :], sd[:, :]).then_inc(rstd_s, 1)
                e.wait_ge(rstd_s, n + 1)
                with e.Fori(0, NT // RING) as i:
                    for p in range(RING):
                        t = i * RING + p
                        e.wait_ge(tr_s, n * NT + t + 1)
                        if n != 1:
                            e.wait_ge(rem_s1, 2 * ((n // 2) * NT + t + 1))
                        else:
                            e.wait_ge(rem_s1, 2 * (NT + RING))
                        e.tensor_scalar(xs[p][:, :], flat(x[:, bass.ds(t, 1), :]), mv[:, bass.ds(t, 1), 0],
                                        rstd[:, bass.ds(t, 1)], ALU.subtract, ALU.mult).then_inc(xs_s, 1)

            def route(k):
                r0 = 5 * k
                lg = ps[:, 2, :].rearrange("p (t e) -> p t e", t=NT)
                pos = ps[:, 3, :].rearrange("p (t e) -> p t e", t=NT)
                bc = lambda a: a[:, :].unsqueeze(2).broadcast_to([P, NT, E])
                e.wait_ge(lg_s, NT * (k + 1) + RING)
                e.tensor_reduce(negmax[:, :], lg, AX.X, ALU.max).then_inc(r_s, 1)
                e.wait_ge(r_s, r0 + 1)
                e.tensor_tensor(zl[:, :, :], lg, bc(negmax), ALU.subtract).then_inc(r_s, 1)
                e.wait_ge(ez_s, k + 1)
                e.tensor_reduce(den[:, :], zl[:, :, :], AX.X, ALU.add).then_inc(r_s, 1)
                e.wait_ge(r_s, r0 + 3)
                e.reciprocal(rden[:, :], den[:, :]).then_inc(r_s, 1)
                e.wait_ge(r_s, r0 + 4)
                e.tensor_tensor(pr[:, :, :], zl[:, :, :], bc(rden), ALU.mult).then_inc(r_s, 1)
                e.wait_ge(r_s, r0 + 5)
                for t in range(NT):
                    e.max(t8[:, t, :], pr[:, t, :]).then_inc(tmax, 1)
                e.wait_ge(tmax, NT * (k + 1))
                for t in range(NT):
                    e.match_replace(rep[:, t, :], t8[:, t, :], pr[:, t, :], -1.0).then_inc(trep, 1)
                e.wait_ge(trep, NT * (k + 1))
                q0 = 8 * k
                e.tensor_scalar(maskb[:, :, :], rep[:, :, :], 0.0, None, ALU.is_lt).then_inc(r2_s, 1)
                e.tensor_reduce(den[:, :], t8[:, :, :], AX.X, ALU.add).then_inc(r2_s, 1)
                e.wait_ge(r2_s, q0 + 2)
                e.reciprocal(rden[:, :], den[:, :]).then_inc(r2_s, 1)
                e.tensor_tensor(wr[:, :, :], pr[:, :, :], maskb[:, :, :], ALU.mult).then_inc(r2_s, 1)
                e.wait_ge(r2_s, q0 + 4)
                e.scalar_tensor_tensor(out=pr[:, :, :], in0=wr[:, :, :], scalar=0.25, in1=bc(rden), op0=ALU.mult, op1=ALU.mult).then_inc(r2_s, 1)
                e.wait_ge(r2_s, q0 + 5)
                e.wait_ge(tok_b, 2 * (k + 1))
                e.tensor_copy(info[:, :, :, 2], pr[:, :, :]).then_inc(r2_s, 1)
                e.wait_ge(r2_s, q0 + 6)
                e.tensor_tensor(wr[:, :, :], pr[:, :, :], info[:, :, :, 2], ALU.subtract).then_inc(r2_s, 1)
                e.wait_ge(r2_s, q0 + 7)
                e.tensor_copy(info[:, :, :, 3], wr[:, :, :]).then_inc(r2_s, 1)
                e.wait_ge(r2_s, q0 + 8)
                e.tensor_tensor(info[:, :, :, 4], wr[:, :, :], info[:, :, :, 3], ALU.subtract).then_inc(posm_s, 1)
                e.tensor_scalar(zl[:, :, :], rep[:, :, :], 0.0, UNROUTED, ALU.is_ge, ALU.mult).then_inc(posm_s, 1)
                e.wait_ge(posm_s, 3 * k + 2)
                e.wait_ge(pos_s, k + 1)
                e.tensor_tensor(posm[:, :, :], pos, zl[:, :, :], ALU.add).then_inc(posm_s, 1)
                e.wait_ge(posm_s, 3 * k + 3)

            def experts(k):
                with e.Fori(0, NCH // RING) as i:
                    for p in range(RING):
                        cl = i * RING + p
                        c = k * NCH + cl
                        with e.Fori(0, NT) as t:
                            e.wait_ge(ga_s, c * NT + t + 1)
                            for q in range(CE):
                                last = e.tensor_scalar(onehot[:, bass.ds(t, 1), q, :].rearrange("p o c -> p (o c)"), iotab[:, :],
                                                       posm[:, bass.ds(t, 1), bass.ds(cl * CE + q, 1)].rearrange("p a b -> p (a b)"),
                                                       None, ALU.is_equal)
                            last.then_inc(oh_s, 1)
                        e.wait_ge(gc_s, c + 1)
                        e.tensor_copy(idx[:, :, 0:5], ps[:, 3, 0:CE * 8].rearrange("p (e w) -> p e w", w=8)[:, :, 0:5]).then_inc(idx_s, 1)
                        e.wait_ge(idx_s, c + 2)
                        e.scalar_tensor_tensor(out=tok[:, :], in0=idx[:, :, 1], scalar=float(P), in1=idx[:, :, 0],
                                               op0=ALU.mult, op1=ALU.add).then_inc(tok_c, 1)
                        e.tensor_tensor(wtmp[:, :], idx[:, :, 2], idx[:, :, 3], ALU.add).then_inc(tok_c, 1)
                        e.wait_ge(tok_c, 2 * c + 2)
                        e.tensor_tensor(wslot[p][:, :], wtmp[:, :], idx[:, :, 4], ALU.add).then_inc(ws_s, 1)
                        e.wait_ge(th_s, c + 1)
                        e.scalar_tensor_tensor(out=flat(ga[:, :, :]), in0=flat(th[:, :, :]), scalar=1.0, in1=ps[0:F, 1, :],
                                               op0=ALU.add, op1=ALU.mult).then_inc(sl_s, 1)
                        e.wait_ge(sl_s, 2 * c + 2)
                        e.tensor_tensor(flat(hT[:, :, :]), flat(ga[:, :, :]), ps[0:F, 2, :], ALU.mult).then_inc(sl_s, 1)
                        e.wait_ge(eoh_s, c + 1)
                        e.wait_ge(ws_s, c + 1)
                        for q in range(CE):
                            last = e.scalar_tensor_tensor(out=eol[p][:, q, :], in0=ps[:, 1, q * D:(q + 1) * D], scalar=wslot[p][:, q:q + 1],
                                                          in1=eoh[p][:, q, :], op0=ALU.mult, op1=ALU.subtract)
                        last.then_inc(eol_s, 1)
                        for q in range(CE):
                            e.wait_ge(q1_free, (c + 2) * CE + q + 1 - RING)
                            e.tensor_scalar(Q1[q % RING][:, :], iota_s[:, :], tok[:, q:q + 1], None, ALU.is_equal).then_inc(q1_s, 1)

            def add_to_x(n):
                for t in range(NT):
                    e.wait_ge(yt_s if n != 1 else wo_s, (n // 2) * NT + t + 1 if n != 1 else t + 1 + RING)
                    bank = t % 2 if n != 1 else 2 + t % 2
                    e.tensor_tensor(x[:, t, :], x[:, t, :], ps[:, bank, 0:D], ALU.add).then_inc(xa_s, 1)
                e.wait_ge(xa_s, NT * (n + 1) + RING)

            e.sem_inc(xa_s, RING)
            e.wait_ge(consts_b, 5)
            e.wait_ge(x_in_s, 16)
            layernorm(0)
            route(0)
            experts(0)
            add_to_x(0)
            layernorm(1)

            for side in range(2):
                for c in range(N // BANK):
                    u = side * (N // BANK) + c
                    e.wait_ge(np_s, u + 1)
                    if u >= RING:
                        e.wait_ge(nh_st[u % RING], 48 * (u // RING))
                    e.tensor_copy(nh[u % RING][:, :], ps[:, 2 + u % 2, :]).then_inc(nh_s, 1)
                    e.wait_ge(nh_s, u + 1)
                    e.tensor_tensor(nl[u % RING][:, :], ps[:, 2 + u % 2, :], nh[u % RING][:, :], ALU.subtract).then_inc(nl_s, 1)
                    e.wait_ge(rp_s, u + 1)
                    cols = slice(c % (T // BANK) * BANK, (c % (T // BANK) + 1) * BANK)
                    e.tensor_tensor(ra[:, :], ps[0:ROPE3, 4, :], cs[:, 0, cols], ALU.mult).then_inc(rp_a, 1)
                    e.tensor_tensor(rb[:, :], ps[0:ROPE3, 5, :], cs[:, 1, cols], ALU.mult).then_inc(rp_b, 1)
                    e.wait_ge(rp_a, 2 * u + 1)
                    e.wait_ge(rp_b, u + 1)
                    e.tensor_tensor(ra[:, :], ra[:, :], rb[:, :], ALU.add).then_inc(rp_a, 1)
                    e.wait_ge(rp_a, 2 * u + 2)
                    dst = (Kst if side == 0 else Qst)[0][0][:, c * BANK:(c + 1) * BANK]
                    e.tensor_copy(dst[0:ROPE3], ra[:, :]).then_inc(rp_h, 1)
                    e.wait_ge(rp_h, u + 1)
                    low = slice(DR, 2 * DR) if side == 0 else slice(2 * DR, 3 * DR)
                    e.tensor_tensor(dst[low], ra[low, :], dst[low], ALU.subtract).then_inc(rp_l, 1)
            for c in range(4):
                e.wait_ge(v_s, c + 1)
                e.tensor_copy(V[:, 4 * c:4 * c + 4, :, :].rearrange("p a b c -> p (a b c)"), ps[:, 6 + c % 2, :]).then_inc(v_c, 1)

            with e.Fori(0, NPAIR // RING) as i:
                for p in range(RING):
                    pair = i * RING + p
                    e.wait_ge(mxt_s, pair + 1)
                    for jt in range(TB):
                        for q in range(4):
                            b, h = q // 2, q % 2
                            u = pair * 4 * TB + jt * 4 + q
                            e.wait_ge(mS_s, u + 1 + 8 * TB)
                            col = h * NT + b * TB + jt
                            src = ps[:, 2 * (q % 2):2 * (q % 2) + 2, :].rearrange("p a b -> p (a b)")[:, 0:(jt + 1) * P]
                            e.tensor_reduce(mx[:, col:col + 1], src, AX.X, ALU.max).then_inc(mx_s, 1)

            with e.Fori(0, NPAIR // RING) as i:
                for p in range(RING):
                    pair = i * RING + p
                    for j in range(2):
                        done = sum(1 for (jj, _) in STEPS if jj <= j)
                        u = pair * 2 + j
                        e.wait_ge(pr_free, (pair + 2) * NS + done)
                        e.tensor_copy(oS[j][:, :], ps[:, 4 + j, :]).then_inc(oS_s, 1)
                        e.wait_ge(ot_s, u + 1)
                        o = ps[:, 6, :].rearrange("p (t s c) -> p t s c", t=4, s=4)
                        e.reciprocal(ord_[:, :, :], o[:, :, :, HD]).then_inc(or_s, 1)
                        e.wait_ge(or_s, u + 1)
                        for b in range(B):
                            dst = attn[:, b * TB + 4 * j:b * TB + 4 * j + 4, bass.ds(pair * 2 * HD, 2 * HD)].rearrange("p t (h c) -> p t h c", h=2)
                            last = e.tensor_tensor(dst, o[:, :, 2 * b:2 * b + 2, 0:HD],
                                                   ord_[:, :, 2 * b:2 * b + 2].unsqueeze(3).broadcast_to([P, 4, 2, HD]), ALU.mult)
                        last.then_inc(om_s, 1)
            add_to_x(1)
            layernorm(2)
            route(1)
            experts(1)
            add_to_x(2)

        @blk.tensor
        def _(e):
            e.wait_ge(consts_in, 48)
            e.wait_ge(gate_in, 16)
            e.transpose(ps[:, 2, 0:E], gate_n[:, :], ident[0:E, 0:E]).then_inc(gate_t, 1)
            e.sem_inc(w_tr, RING)
            with e.Fori(0, NCH // RING) as i:
                for p in range(RING):
                    c = i * RING + p
                    e.wait_ge(w_nat[p], 32 * (i + 1))
                    e.wait_ge(w_c1, c + 1)
                    e.wait_ge(w_c2, c + 1)
                    for q in range(2 * CE):
                        bank, col = 3 + q // CE, (q % CE) * F
                        e.transpose(ps[:, bank, col:col + F], wgn[p][:, q, :], ident[0:F, 0:F])
                    for q in range(CE):
                        last = e.transpose(ps[0:F, 5, q * D:(q + 1) * D], wdn[p][:, q, :], ident[:, :])
                    last.then_inc(w_tr, 1)

            def transposes(n):
                with e.Fori(0, NT // RING) as i:
                    for p in range(RING):
                        u = n * NT + i * RING + p
                        e.wait_ge(xs_s, u + 1)
                        e.wait_ge(xt_s, u + 1)
                        e.transpose(ps[:, p, 0:P], xs[p][:, :], ident[:, :]).then_inc(tr_s, 1)
                    if n != 1:
                        for p in range(RING):
                            t = i * RING + p
                            e.wait_ge(xt_s, n * NT + t + 1 + RING)
                            e.matmul(ps[:, 2, bass.ds(t * E, E)], xt[p][:, :], gateT[:, :], start=True, stop=True).then_inc(lg_s, 1)

            def positions(k):
                e.wait_ge(r2_s, 8 * k + 1)
                e.matmul(ps[:, 3, :], zerosb[:, 0:P], zerosb[:, :], start=True, stop=False, skip_group_check=True)
                for t in range(NT - 1):
                    o = ps[:, 3, (t + 1) * E:].rearrange("p (t e) -> p t e", e=E)
                    e.matmul(o, onesb[:, :], maskb[:, t:t + 1, :].broadcast_to([P, NT - 1 - t, E]),
                             start=False, stop=False, skip_group_check=True)
                e.matmul(ps[:, 3, :], tri[:, :], flat(maskb[:, :, :]), start=False, stop=True, skip_group_check=True).then_inc(pos_s, 1)

            def experts(k):
                e.wait_ge(posm_s, 3 * (k + 1))
                e.wait_ge(xp_s, NT * (k + 1))
                for j in range(4):
                    e.matmul(ps[:, 4 + j, :], zerosb[:, 0:P], zerosb[:, :], start=True, stop=False, skip_group_check=True)
                with e.Fori(0, NCH // RING) as i:
                    for p in range(RING):
                        cl = i * RING + p
                        c = k * NCH + cl
                        e.wait_ge(bufT_s, c + 1)
                        e.wait_ge(idx_s, c + 1)
                        e.matmul(ps[:, 0, :], zerosb[:, 0:P], zerosb[:, :], start=True, stop=False, skip_group_check=True)
                        e.matmul(ps[:, 3, 0:CE * 8], zerosb[:, 0:P], zerosb[:, 0:CE * 8], start=True, stop=False, skip_group_check=True)
                        with e.Fori(0, NT) as t:
                            e.wait_ge(oh_s, c * NT + t + 1)
                            for part in range(3):
                                e.matmul(ps[:, 0, :], xp[:, bass.ds(t, 1), part, :].rearrange("p o d -> p (o d)"),
                                         onehot[:, bass.ds(t, 1), :, :].rearrange("p o e c -> p (o e c)"),
                                         start=False, stop=False, skip_group_check=True)
                            for q in range(CE):
                                last = e.matmul(ps[:, 3, q * 8:q * 8 + 5], onehot[:, bass.ds(t, 1), q, :].rearrange("p o c -> p (o c)"),
                                                info[:, bass.ds(t, 1), bass.ds(cl * CE + q, 1), :].rearrange("p a b w -> p (a b w)"),
                                                start=False, stop=False, skip_group_check=True)
                            last.then_inc(ga_s, 1)
                        for bank, w in ((0, BANK), (3, CE * 8)):
                            last = e.matmul(ps[:, bank, 0:w], zerosb[:, 0:P], zerosb[:, 0:w], start=False, stop=True, skip_group_check=True)
                        last.then_inc(gc_s, 1)
                        e.wait_ge(bufT_s, c + 2)
                        e.wait_ge(gus_in[p], 16 * (k * NCH // RING + i + 1))
                        if True:
                            e.wait_ge(eol_s, c + 1)
                        for half, bank in ((0, 1), (1, 2)):
                            for q in range(CE):
                                last = e.matmul(ps[0:F, bank, q * CAP:(q + 1) * CAP], gus[p][:, q, half, :], bufT[p][:, q, :], start=True, stop=True)
                        last.then_inc(gu_s, 1)
                        e.wait_ge(sl_s, 2 * c + 3)
                        e.wait_ge(dns_in[p], 16 * (k * NCH // RING + i + 1))
                        for q in range(CE):
                            last = e.matmul(ps[:, 1, q * D:(q + 1) * D], hT[:, q, :], dns[p][:, q, :], start=True, stop=True)
                        last.then_inc(eo_s, 1)
                        e.wait_ge(eoh_s, c + 1)
                        e.wait_ge(eol_s, c + 2)
                        for q in range(CE):
                            e.wait_ge(q1_s, c * CE + q + 1)
                            for w in (eoh, eol):
                                for j in range(4):
                                    last = e.matmul(ps[:, 4 + j, :], w[p][:, q, :], Q1[q % RING][:, j * BANK:(j + 1) * BANK],
                                                    start=False, stop=False, skip_group_check=True)
                            last.then_inc(q1_free, 1)
                for j in range(4):
                    last = e.matmul(ps[:, 4 + j, :], zerosb[:, 0:P], zerosb[:, :], start=False, stop=True, skip_group_check=True)
                last.then_inc(y_s, 1)
                e.wait_ge(yT_s, k + 1)
                for t in range(NT):
                    e.wait_ge(xa_s, 2 * k * NT + t + 1)
                    e.transpose(ps[:, t % 2, 0:P], yT[:, t * P:(t + 1) * P], ident[:, :]).then_inc(yt_s, 1)

            e.sem_inc(tr_s, RING)
            e.sem_inc(lg_s, RING)
            e.sem_inc(ga_s, NT)
            e.sem_inc(gu_s, RING)
            e.sem_inc(q1_free, 2 * CE)
            e.wait_ge(consts_b, 5)
            e.wait_ge(zeros_b, 2)
            e.wait_ge(gate_c, 1)
            transposes(0)
            positions(0)
            experts(0)
            transposes(1)

            e.wait_ge(xt_s, 2 * NT + RING)
            e.wait_ge(watt_in, 16 * 9)
            for c in range(N // BANK):
                if c >= 2:
                    e.wait_ge(ckv_c, c - 1)
                e.matmul(ps[:, c % 2, :], wat[:, 0, :], xnT[:, c * BANK:(c + 1) * BANK], start=True, stop=True).then_inc(ckv_s, 1)
            e.wait_ge(ckv_c, N // BANK)
            e.wait_ge(wrep_s, 6)
            for side in range(2):
                src, w = ((ckvT, 1), (xnT, 3))[side]
                for c in range(N // BANK):
                    u = side * (N // BANK) + c
                    cols = slice(c * BANK, (c + 1) * BANK)
                    if u >= 2:
                        e.wait_ge(nl_s, u - 1)
                    e.matmul(ps[:, 2 + u % 2, :], wat[:, w, :], src[:, cols], start=True, stop=True).then_inc(np_s, 1)
                    if u >= 1:
                        e.wait_ge(rp_b, u)
                    for v in range(2):
                        last = e.matmul(ps[0:ROPE3, 4 + v, :], wrep[:, side, v, :, :].rearrange("p r d -> p (r d)"), src[:, cols], start=True, stop=True)
                    last.then_inc(rp_s, 1)
            for c in range(4):
                if c >= 2:
                    e.wait_ge(v_c, c - 1)
                for q in range(4):
                    t = 4 * c + q
                    last = e.matmul(ps[:, 6 + c % 2, q * P:(q + 1) * P], ckvT[:, t * P:(t + 1) * P], wat[:, 2, :], start=True, stop=True)
                last.then_inc(v_s, 1)

            e.wait_ge(ropek, 16 * 6)
            e.wait_ge(nl_s, 2 * N // BANK)
            e.wait_ge(v_c, 4)
            e.sem_inc(mS_s, 8 * TB)
            e.sem_inc(mx_s, RING)
            with e.Fori(0, NPAIR // RING) as i:
                for p in range(RING):
                    pair = i * RING + p
                    e.wait_ge(kst_in[p], 64 * (i + 1))
                    for jt in range(TB):
                        for q in range(4):
                            b, h = q // 2, q % 2
                            u = pair * 4 * TB + jt * 4 + q
                            e.wait_ge(mx_s, u + 1)
                            width = (jt + 1) * P
                            for o in range(0, width, BANK):
                                w = min(BANK, width - o)
                                bank = 2 * (q % 2) + o // BANK
                                e.matmul(ps[:, bank, 0:w], Qst[p][h][0:ROWS, b * T + jt * P:b * T + (jt + 1) * P],
                                         Kst[p][h][0:ROWS, b * T + o:b * T + o + w], start=True, stop=False, skip_group_check=True)
                            last = e.matmul(ps[:, bank, w - P:w], identb[:, :], maskQ[:, :], start=False, stop=True, skip_group_check=True)
                            last.then_inc(mS_s, 1)
                    e.wait_ge(mx_s, 4 * TB * (pair + 1) + RING)
                    e.wait_ge(shf_s, pair + 1)
                    e.transpose(ps[0:2 * NT, 6, 0:P], mx[:, :], ident[:, :]).then_inc(mxt_s, 1)

            e.sem_inc(pr_s, RING)
            e.sem_inc(pr_free, 2 * NS)
            e.sem_inc(st_ready, 4 * NS)
            e.sem_inc(oS_s, 2)
            with e.Fori(0, NPAIR // RING) as i:
                for p in range(RING):
                    pair = i * RING + p
                    e.wait_ge(kst_in[p], 32 * NPAIR + 96 * (i + 1))
                    e.wait_ge(vst_s, pair + 1)
                    e.wait_ge(vst_z, 2 * RING)

                    def scores(n):
                        j, kt = STEPS[n]
                        lo = max(0, kt * P - j * BANK)
                        diagonal = kt * P >= j * BANK
                        for b in range(B):
                            e.wait_ge(pr_s, pair * 2 * NS + 2 * n + b + 1)
                            for h in range(2):
                                last = e.matmul(ps[:, 2 * b + h, lo:BANK], Kst[p][h][0:ROWS + 1, b * T + kt * P:b * T + (kt + 1) * P],
                                                Qst[p][h][0:ROWS + 1, b * T + j * BANK + lo:b * T + (j + 1) * BANK],
                                                start=True, stop=not diagonal, skip_group_check=True)
                                if diagonal:
                                    last = e.matmul(ps[:, 2 * b + h, lo:lo + P], identb[:, :], maskT[:, :], start=False, stop=True, skip_group_check=True)
                            last.then_inc(st_ready, 1)

                    def weighted(n):
                        j, kt = STEPS[n]
                        lo = max(0, kt * P - j * BANK)
                        e.wait_ge(pr_s, pair * 2 * NS + 2 * n + 2 + RING)
                        if kt == 0:
                            e.wait_ge(oS_s, pair * 2 + j + 1)
                        for q in range(4):
                            b, h = q // 2, q % 2
                            last = e.matmul(ps[VW * q:VW * (q + 1), 4 + j, lo:BANK], Vst[p][:, b * TB + kt, h, :], probs[n % RING][:, q, lo:BANK],
                                            start=(kt == 0), stop=(kt == (j + 1) * BANK // P - 1), skip_group_check=True)
                        last.then_inc(pr_free, 1)

                    def turn(j):
                        u = pair * 2 + j
                        e.wait_ge(oS_s, u + 1 + 2)
                        e.wait_ge(om_s, u + 1)
                        for q in range(4):
                            last = e.transpose(ps[:, 6, q * P:(q + 1) * P], oS[j][:, q * P:(q + 1) * P], ident[:, :])
                        last.then_inc(ot_s, 1)

                    scores(0)
                    for n in range(NS):
                        if n + 1 < NS:
                            scores(n + 1)
                        weighted(n)
                        if n == 6:
                            turn(0)
                    turn(1)

            e.wait_ge(om_s, 2 * NPAIR + 1)
            e.sem_inc(wo_s, RING)
            for t in range(NT + 1):
                if t < NT:
                    if t >= 2:
                        e.wait_ge(at_c, t - 1)
                    e.transpose(ps[:, t % 2, 0:P], attn[:, t, :], ident[:, :]).then_inc(at_s, 1)
                if t >= 1:
                    e.wait_ge(at_c, t)
                    e.wait_ge(xa_s, NT + t)
                    e.matmul(ps[:, 2 + (t - 1) % 2, 0:D], attnT[(t - 1) % RING][:, :], wat[:, 4, :], start=True, stop=True).then_inc(wo_s, 1)
            e.wait_ge(xa_s, 2 * NT + RING)
            transposes(2)
            positions(1)
            experts(1)


_INS = ['L0_attn_x', 'L0_attn_W_kv_down', 'L0_attn_W_k_up', 'L0_attn_W_v_up', 'L0_attn_W_q', 'L0_attn_W_q_rope',
        'L0_attn_W_k_rope', 'L0_attn_W_o', 'L0_ffn_gate_weight', 'L0_ffn_gate_up_proj', 'L0_ffn_down_proj']


def constants():
    a = np.arange(P)
    before = (a[:, None] < a[None, :]).astype(np.float32)
    masked = np.float32(MASKED)
    squares = np.stack([np.eye(P, dtype=np.float32), before, masked * before.T, masked * before])
    inv_freq = np.float32(1.0) / np.power(np.float32(10000.0), np.arange(0, DR, 2, dtype=np.float32) / np.float32(DR))
    angle = (np.arange(T, dtype=np.float32)[None, :] * inv_freq.astype(np.float32)[:, None]).astype(np.float32)
    c, s = np.cos(angle), np.sin(angle)
    return {
        "squares": squares.astype(np.float32),
        "cos3": np.tile(np.concatenate([c, c]), (3, 1)).astype(np.float32),
        "sin3": np.tile(np.concatenate([-s, s]), (3, 1)).astype(np.float32),
        "iota": np.arange(N, dtype=np.float32)[None, :],
        "tokinfo": np.stack(np.broadcast_arrays(a[:, None], np.arange(NT)[None, :]), -1).astype(np.float32),
    }


def kernel(**inputs):
    from concourse import bacc
    from concourse.bass_utils import run_bass_kernel_spmd

    nc = bacc.Bacc("TRN2", target_bir_lowering=False, num_devices=1)
    arrays, args = {}, []
    given = {n: np.ascontiguousarray(inputs[n]) for n in _INS}
    for name, a in {**given, **constants()}.items():
        arrays[f"in_{name}"] = a
        args.append(nc.dram_tensor(f"in_{name}", a.shape, mybir.dt.from_np(a.dtype), kind="ExternalInput").ap())
    args.append(nc.dram_tensor("out_0", (B, T, D), F32, kind="ExternalOutput").ap())
    build(nc, *args)
    r = run_bass_kernel_spmd(nc, [arrays], core_ids=[0])
    return r.results[0]["out_0"]
```

```python
from contextlib import ExitStack

import numpy as np
import concourse.bass as bass
from concourse import mybir

F32 = mybir.dt.float32
F32R = mybir.dt.float32r
BF16 = mybir.dt.bfloat16
ALU = mybir.AluOpType
ACT = mybir.ActivationFunctionType
AX = mybir.AxisListType

P = 128
B, T, D = 2, 1024, 128
N = B * T
NT = N // P
TB = T // P
NH, HD, DR = 16, 8, 32
E, F, TOPK, CAP = 32, 96, 8, 128
CE = 4
NCH = E // CE
BANK = 512
NPAIR = NH // 2
ROPE3 = 3 * DR
NOPE3 = 3 * HD
ROWS = ROPE3 + NOPE3
VW = 32
SCALE = 1.0 / float(np.sqrt(HD + DR))
EPS = 1e-5
UNROUTED = 4096.0
MASKED = -1e30
NG = 4
TG = NT // NG
NEAR = 768
RING = 2

STEPS = [(j, i) for j in range(T // BANK) for i in range((j + 1) * BANK // P)]
NS = len(STEPS)
UNITS = [(jt, o, q) for jt in range(TB) for o in range(0, (jt + 1) * P, BANK) for q in range(4)]
NU = len(UNITS)
U0, US = 2, 6
NC = N // BANK


def build(nc, x_in, w_kv_down, w_k_up, w_v_up, w_q, w_q_rope, w_k_rope, w_o,
          gate_weight, gate_up_proj, down_proj, squares, cos3, sin3, iota, tokinfo, out):
    ctx = ExitStack()

    def sb(name, shape, dt=F32, stack=None):
        return (stack or ctx).enter_context(nc.sbuf_tensor(name, shape, dt))

    def sem(name):
        return ctx.enter_context(nc.semaphore(name))

    def flat(a):
        return a.rearrange("p a b -> p (a b)")

    def flat3(a):
        return a.rearrange("p a b c -> p (a b c)")

    def raw(a):
        return a.bitcast(F32)

    with ctx:
        guT_d = nc.dram_tensor("guT_d", [NCH, P, CE * 2 * F], F32).ap()
        dnT_d = nc.dram_tensor("dnT_d", [NCH, F, CE * D], F32).ap()
        kn_d = nc.dram_tensor("kn_d", [3, NH * HD, N], F32).ap()
        qn_d = nc.dram_tensor("qn_d", [3, NH * HD, N], F32).ap()

        x = sb("x", [P, NT, D])
        xn = sb("xn", [P, NT, D])
        xnT = sb("xnT", [D, N])
        sq = sb("sq", [P, 4, P])
        ident = sq[:, 0, :]
        identb = sb("identb", [P, P], BF16)
        beforeb = sb("beforeb", [P, P], BF16)
        maskT = sb("maskT", [P, P], BF16)
        maskQ = sb("maskQ", [P, P], BF16)
        onesb = sb("onesb", [P, P], BF16)
        zerosb = sb("zerosb", [P, BANK], BF16)
        gate_n = sb("gate_n", [E, D])
        gateT = sb("gateT", [D, E])
        iota_s = sb("iota_s", [P, N])
        iotab = sb("iotab", [P, P], BF16)
        tokinfo_s = sb("tokinfo_s", [P, NT, 2])
        stats = sb("stats", [P, NT, 6])
        mv = sb("mv", [P, NT, 2])
        var = sb("var", [P, NT])
        sd = sb("sd", [P, NT])
        rstd = sb("rstd", [P, NT])
        wat = sb("wat", [P, 5, D])
        wrope = sb("wrope", [P, 2, DR])
        wrep = sb("wrep", [P, 2, 2, 3, DR])
        gus = [sb(f"gus{p}", [P, CE, 2, F]) for p in range(RING)]
        dns = [sb(f"dns{p}", [F, CE, D]) for p in range(RING)]

        moe = ExitStack()
        wgn = [sb(f"wgn{p}", [F, CE * 2, D], F32, moe) for p in range(RING)]
        wdn = [sb(f"wdn{p}", [D, CE, F], F32, moe) for p in range(RING)]
        xp = sb("xp", [P, NT, 3, D], BF16, moe)
        rem = [sb(f"rem{p}", [P, TG, D], F32, moe) for p in range(RING)]
        top = sb("top", [P, NT], F32, moe)
        zl = sb("zl", [P, NT, E], F32, moe)
        pr = sb("pr", [P, NT, E], F32, moe)
        den = sb("den", [P, NT], F32, moe)
        rden = sb("rden", [P, NT], F32, moe)
        t8 = sb("t8", [P, NT, TOPK], F32, moe)
        rep = sb("rep", [P, NT, E], F32, moe)
        maskb = sb("maskb", [P, NT, E], BF16, moe)
        wr = sb("wr", [P, NT, E], F32, moe)
        info = sb("info", [P, NT, E, 5], BF16, moe)
        posm = sb("posm", [P, NT, E], F32, moe)
        least = sb("least", [1, NT], F32, moe)
        nactf = sb("nactf", [1, 1], F32, moe)
        nact = sb("nact", [1, 1], mybir.dt.int32, moe)
        onehot = sb("onehot", [P, NT, CE, CAP], BF16, moe)
        bufT = [sb(f"bufT{p}", [D, CE, CAP], F32, moe) for p in range(RING)]
        idx = sb("idx", [P, CE, 8], F32, moe)
        tok = [sb(f"tok{p}", [P, CE], F32, moe) for p in range(RING)]
        wslot = [sb(f"wslot{p}", [P, CE], F32, moe) for p in range(RING)]
        wtmp = sb("wtmp", [P, CE], F32, moe)
        th = sb("th", [F, CE, CAP], F32, moe)
        ga = sb("ga", [F, CE, CAP], F32, moe)
        hT = sb("hT", [F, CE, CAP], F32, moe)
        eoh = [sb(f"eoh{p}", [P, CE, D], F32R, moe) for p in range(RING)]
        eol = [sb(f"eol{p}", [P, CE, D], F32R, moe) for p in range(RING)]
        place = [sb(f"place{q}", [P, N], F32R, moe) for q in range(CE)]
        yT = sb("yT", [D, N], F32, moe)
        moe.close()

        att = ExitStack()
        ckvT = sb("ckvT", [D, N], F32, att)
        cs = sb("cs", [ROPE3, 2, T], F32, att)
        ra = [sb(f"ra{p}", [ROPE3, BANK], F32, att) for p in range(RING)]
        rb = [sb(f"rb{p}", [ROPE3, BANK], F32, att) for p in range(RING)]
        nh = [sb(f"nh{p}", [P, BANK], F32R, att) for p in range(RING)]
        nl = [sb(f"nl{p}", [P, BANK], F32R, att) for p in range(RING)]
        V = sb("V", [P, NT, NH, HD], F32, att)
        Vst = [sb(f"Vst{p}", [P, NT, 2, VW], F32, att) for p in range(RING)]
        Kst = [[sb(f"Kst{p}{h}", [P, N], F32R, att) for h in range(2)] for p in range(RING)]
        Qst = [[sb(f"Qst{p}{h}", [P, N], F32R, att) for h in range(2)] for p in range(RING)]
        probs = [sb(f"probs{p}", [P, 4, BANK], F32, att) for p in range(RING)]
        mxh = sb("mxh", [P, 2, 2 * NT], F32, att)
        mx = sb("mx", [P, 2 * NT], F32, att)
        shf = sb("shf", [2 * NT, P], F32R, att)
        oS = [sb(f"oS{j}", [P, BANK], F32, att) for j in range(2)]
        ord_ = sb("ord", [P, 4, 4], F32, att)
        att.close()
        attn = xn

        ps = ctx.enter_context(nc.psum_tensor("ps", [P, 8, BANK], F32))

        x_in_s, gate_in, consts_in, watt_in, cs_in = (sem(n) for n in ("x_in_s", "gate_in", "consts_in", "watt_in", "cs_in"))
        bf_consts, memsets, rope_weights = (sem(n) for n in ("bf_consts", "memsets", "rope_weights"))
        gate_turned, gate_copied = sem("gate_turned"), sem("gate_copied")
        nat_in = [sem(f"nat_in{p}") for p in range(RING)]
        w_turned, w_copied = sem("w_turned"), sem("w_copied")
        w_stored = [sem(f"w_stored{p}") for p in range(RING)]
        gus_in = [sem(f"gus_in{p}") for p in range(RING)]
        dns_in = [sem(f"dns_in{p}") for p in range(RING)]
        stat_done, moments, var_ready, sd_ready, rstd_ready, xn_ready = (
            sem(n) for n in ("stat_done", "moments", "var_ready", "sd_ready", "rstd_ready", "xn_ready"))
        turned, xnT_ready, logits_done = sem("turned"), sem("xnT_ready"), sem("logits_done")
        part0, rem1, part1, split_done = sem("part0"), sem("rem1"), sem("part1"), sem("split_done")
        soft, exp_done, top8, replaced, routed, info_const, pos_done, posm_ready, act_step, nact_ready = (
            sem(n) for n in ("soft", "exp_done", "top8", "replaced", "routed", "info_const", "pos_done", "posm_ready",
                             "act_step", "nact_ready"))
        onehot_ready = [sem(f"onehot_ready{k}") for k in range(2)]
        placed_far = [sem(f"placed_far{k}") for k in range(2)]
        gathered, bufT_ready, idx_ready, slot_step, slots_ready, gu_done, th_ready, silu_step, eo_done, eoh_ready, eol_ready = (
            sem(n) for n in ("gathered", "bufT_ready", "idx_ready", "slot_step", "slots_ready", "gu_done", "th_ready",
                             "silu_step", "eo_done", "eoh_ready", "eol_ready"))
        placed, combined, y_done, yT_ready, y_turned, added = (
            sem(n) for n in ("placed", "combined", "y_done", "yT_ready", "y_turned", "added"))
        ckv_done, ckvT_ready, nope_done, nh_ready, nl_ready = (
            sem(n) for n in ("ckv_done", "ckvT_ready", "nope_done", "nh_ready", "nl_ready"))
        nope_stored = [sem(f"nope_stored{p}") for p in range(RING)]
        rope_done, ra_ready, rb_ready, rsum_ready, hi_ready, lo_ready = (
            sem(n) for n in ("rope_done", "ra_ready", "rb_ready", "rsum_ready", "hi_ready", "lo_ready"))
        rope_copied, v_done, v_ready, vst_const, vst_ready, rows_const = (
            sem(n) for n in ("rope_copied", "v_done", "v_ready", "vst_const", "vst_ready", "rows_const"))
        stage_in = [sem(f"stage_in{p}") for p in range(RING)]
        shift_in = [sem(f"shift_in{p}") for p in range(RING)]
        mscores_done, mx_const, mx_ready, mx_joined, mx_turned, shf_ready = (
            sem(n) for n in ("mscores_done", "mx_const", "mx_ready", "mx_joined", "mx_turned", "shf_ready"))
        scores_done, probs_ready, pv_done, oS_ready, o_turned, oden_ready, attn_ready, wo_done, out_s = (
            sem(n) for n in ("scores_done", "probs_ready", "pv_done", "oS_ready", "o_turned", "oden_ready", "attn_ready",
                             "wo_done", "out_s"))

        blk = ctx.enter_context(nc.Block())

        def ring_loop(e, step, first, last):
            with e.Fori(0, (last - first + 1) // RING) as i:
                for q in range(RING):
                    step(i * RING + (first + q), (first + q) % RING, i + (first + q) // RING)

        @blk.sync
        def _(e):
            for g in range(NG):
                b, r = g * TG // TB, g * TG % TB
                e.dma_start(x[:, g * TG:(g + 1) * TG, :], x_in[b, r * P:(r + TG) * P].rearrange("(t p) d -> p t d", p=P)).then_inc(x_in_s, 16)
            e.dma_start(gate_n[:, :], gate_weight).then_inc(gate_in, 16)
            with e.Fori(0, NCH // RING) as i:
                for p in range(RING):
                    c = i * RING + p
                    e.wait_ge(w_turned, c + 1)
                    e.dma_start(wgn[p][:, :, :], gate_up_proj[bass.ds(c * CE, CE)].rearrange("e (s f) h -> f (e s) h", s=2)).then_inc(nat_in[p], 16)
                    e.dma_start(wdn[p][:, :, :], down_proj[bass.ds(c * CE, CE)].rearrange("e h f -> h e f")).then_inc(nat_in[p], 16)
            for n, w in enumerate((w_kv_down, w_k_up, w_v_up, w_q, w_o)):
                e.dma_start(wat[:, n, :], w).then_inc(watt_in, 16)
            e.dma_start(wrope[:, 0, :], w_k_rope).then_inc(watt_in, 16)
            e.dma_start(wrope[:, 1, :], w_q_rope).then_inc(watt_in, 16)

            def stage_weights(k):
                with e.Fori(0, NCH // RING) as i:
                    for p in range(RING):
                        c = i * RING + p
                        e.wait_ge(eo_done, k * NCH + c + 1)
                        e.dma_start(flat3(gus[p][:, :, :, :]), guT_d[bass.ds(c, 1)].rearrange("o p n -> (o p) n")).then_inc(gus_in[p], 16)
                        e.dma_start(flat(dns[p][:, :, :]), dnT_d[bass.ds(c, 1)].rearrange("o p n -> (o p) n")).then_inc(dns_in[p], 16)

            for p in range(RING):
                e.wait_ge(w_stored[p], 16 * NCH)
            stage_weights(0)

            e.wait_ge(added, NG + RING)
            e.dma_start(cs[:, 0, :], cos3).then_inc(cs_in, 16)
            e.dma_start(cs[:, 1, :], sin3).then_inc(cs_in, 16)
            e.wait_ge(rows_const, 8)
            for side, (dst, parts, st) in enumerate(((kn_d, "hlh", Kst), (qn_d, "hhl", Qst))):
                for c in range(NC):
                    u = side * NC + c
                    cols = slice(c * BANK, (c + 1) * BANK)
                    e.wait_ge(nh_ready, u + 1)
                    e.wait_ge(nl_ready, u + 1)
                    for r, part in enumerate(parts):
                        src = nh[u % RING] if part == "h" else nl[u % RING]
                        e.dma_start(dst[r, :, cols], raw(src[:, :])).then_inc(nope_stored[u % RING], 16)
                    e.wait_ge(lo_ready, u + 1)
                    for p, h in ((0, 1), (1, 0), (1, 1)):
                        e.dma_start(raw(st[p][h][0:ROPE3, cols]), raw(st[0][0][0:ROPE3, cols])).then_inc(rope_copied, 16)
            for q in range(RING):
                e.wait_ge(nope_stored[q], 48 * NC)

            def stage_pair(pair, p):
                e.wait_ge(scores_done, 2 * NS * (pair + 1))
                for h in range(2):
                    rows = bass.ds((pair * 2 + h) * HD, HD)
                    e.dma_start(raw(Kst[p][h][ROPE3:ROWS, :]), kn_d[:, rows, :]).then_inc(stage_in[p], 16)
                    e.dma_start(raw(Qst[p][h][ROPE3:ROWS, :]), qn_d[:, rows, :]).then_inc(stage_in[p], 16)

            def stage_shift(pair, p):
                e.wait_ge(shf_ready, pair + 2)
                for h in range(2):
                    e.dma_start(raw(Qst[p][h][ROWS:ROWS + 1, :]), raw(shf[h * NT:(h + 1) * NT, :])).then_inc(shift_in[p], 16)

            def pair_step(pair, p, h):
                stage_pair(pair, p)
                stage_shift(pair, p)

            pair_step(0, 0, 0)
            pair_step(1, 1, 0)
            ring_loop(e, pair_step, 2, NPAIR - 1)
            stage_weights(1)
            for g in range(NG):
                b, r = g * TG // TB, g * TG % TB
                e.wait_ge(added, 2 * NG + g + 1 + RING)
                e.dma_start(out[b, r * P:(r + TG) * P].rearrange("(t p) d -> p t d", p=P), x[:, g * TG:(g + 1) * TG, :]).then_inc(out_s, 16)
            e.wait_ge(out_s, 16 * NG)

        @blk.gpsimd
        def _(e):
            e.sem_inc(w_copied, 1)
            e.sem_inc(idx_ready, 1)
            e.sem_inc(eol_ready, 1)
            e.sem_inc(bufT_ready, 1)
            e.sem_inc(silu_step, 1)
            e.sem_inc(mx_turned, 1)
            e.sem_inc(attn_ready, 1)
            e.sem_inc(shf_ready, 1)
            e.memset(onesb[:, :], 1.0).then_inc(memsets, 1)
            e.memset(zerosb[:, :], 0.0).then_inc(memsets, 1)
            e.wait_ge(consts_in, 48)
            e.tensor_copy(identb[:, :], sq[:, 0, :]).then_inc(bf_consts, 1)
            e.tensor_copy(beforeb[:, :], sq[:, 1, :]).then_inc(bf_consts, 1)
            e.tensor_copy(maskT[:, :], sq[:, 2, :]).then_inc(bf_consts, 1)
            e.tensor_copy(maskQ[:, :], sq[:, 3, :]).then_inc(bf_consts, 1)
            e.tensor_copy(iotab[:, :], iota_s[:, 0:P]).then_inc(bf_consts, 1)

            def split(k):
                for q in range(2):
                    e.tensor_copy(info[:, :, :, q], tokinfo_s[:, :, q:q + 1].broadcast_to([P, NT, E])).then_inc(info_const, 1)
                for g in range(NG):
                    u = k * NG + g
                    t = slice(g * TG, (g + 1) * TG)
                    r = rem[g % RING]
                    e.wait_ge(xn_ready, 2 * k * NT + (g + 1) * TG)
                    e.tensor_copy(xp[:, t, 0, :], xn[:, t, :]).then_inc(part0, 1)
                    e.wait_ge(part0, u + 1)
                    e.tensor_tensor(r[:, :, :], xn[:, t, :], xp[:, t, 0, :], ALU.subtract).then_inc(rem1, 1)
                    e.wait_ge(rem1, u + 1)
                    e.tensor_copy(xp[:, t, 1, :], r[:, :, :]).then_inc(part1, 1)
                    e.wait_ge(part1, u + 1)
                    e.tensor_tensor(xp[:, t, 2, :], r[:, :, :], xp[:, t, 1, :], ALU.subtract).then_inc(split_done, 1)

            def store_weights():
                with e.Fori(0, NCH // RING) as i:
                    for p in range(RING):
                        c = i * RING + p
                        e.wait_ge(w_copied, 2 * c + 3)
                        e.dma_start(guT_d[bass.ds(c, 1)].rearrange("o p n -> (o p) n"), flat3(gus[p][:, :, :, :])).then_inc(w_stored[p], 16)
                        e.dma_start(dnT_d[bass.ds(c, 1)].rearrange("o p n -> (o p) n"), flat(dns[p][:, :, :])).then_inc(w_stored[p], 16)

            split(0)
            store_weights()
            e.wait_ge(watt_in, 16 * 7)
            half = DR // 2
            for side in range(2):
                e.tensor_copy(wrep[:, side, 0, :, :], wrope[:, side:side + 1, :].broadcast_to([P, 3, DR])).then_inc(rope_weights, 1)
                e.tensor_copy(wrep[:, side, 1, :, 0:half], wrope[:, side:side + 1, half:DR].broadcast_to([P, 3, half])).then_inc(rope_weights, 1)
                e.tensor_copy(wrep[:, side, 1, :, half:DR], wrope[:, side:side + 1, 0:half].broadcast_to([P, 3, half])).then_inc(rope_weights, 1)
            e.wait_ge(rope_weights, 6)
            e.wait_ge(added, NG + RING)
            for p in range(RING):
                for h in range(2):
                    e.memset(raw(Kst[p][h][ROPE3:P, :]), 1.0).then_inc(rows_const, 1)
                    e.memset(raw(Qst[p][h][ROPE3:P, :]), 0.0).then_inc(rows_const, 1)
            e.wait_ge(rows_const, 8)
            for p in range(RING):
                e.memset(Vst[p][:, :, :, HD:VW], 0.0).then_inc(vst_const, 1)
            e.wait_ge(vst_const, RING)
            for p in range(RING):
                e.memset(Vst[p][:, :, :, HD:HD + 1], 1.0).then_inc(vst_const, 1)
            e.memset(mxh[:, :, :], MASKED).then_inc(mx_const, 1)
            for u in range(2 * NC):
                r = u % RING
                e.wait_ge(ra_ready, u + 1)
                e.wait_ge(rb_ready, u + 1)
                e.tensor_tensor(ra[r][:, :], ra[r][:, :], rb[r][:, :], ALU.add).then_inc(rsum_ready, 1)
            e.wait_ge(v_ready, NG)
            with e.Fori(0, NPAIR // RING) as i:
                for p in range(RING):
                    pair = i * RING + p
                    e.wait_ge(pv_done, NS * (pair + 1))
                    e.tensor_copy(Vst[p][:, :, :, 0:HD], V[:, :, bass.ds(pair * 2, 2), :]).then_inc(vst_ready, 1)
            e.wait_ge(vst_ready, NPAIR)
            e.wait_ge(wo_done, 1)
            split(1)

        @blk.scalar
        def _(e):
            e.dma_start(sq[:, :, :], squares.rearrange("k p c -> p k c")).then_inc(consts_in, 16)
            e.dma_start(tokinfo_s[:, :, :], tokinfo).then_inc(consts_in, 16)
            e.dma_start(iota_s[:, :], iota.broadcast_to([P, N])).then_inc(consts_in, 16)
            e.sem_inc(xnT_ready, RING)

            def transposed(n, norm=True):
                if norm:
                    e.wait_ge(var_ready, n - n // 3 + 1)
                    e.activation(sd[:, :], var[:, :], ACT.Sqrt).then_inc(sd_ready, 1)
                for g in range(NG):
                    e.wait_ge(turned, n * NG + g + 1)
                    e.activation(xnT[:, g * BANK:(g + 1) * BANK], ps[:, g % RING, :], ACT.Copy).then_inc(xnT_ready, 1)

            def exps(k):
                e.wait_ge(soft, 2 + 5 * k)
                e.activation(zl[:, :, :], zl[:, :, :], ACT.Exp).then_inc(exp_done, 1)

            def experts(k):
                def gather_out(c, p):
                    e.wait_ge(gathered, k * NCH + c + 1)
                    e.wait_ge(gu_done, k * NCH + c + 1)
                    e.activation(flat(bufT[p][:, :, :]), ps[:, 0, :], ACT.Copy).then_inc(bufT_ready, 1)

                def step(c, p, h=0, last=False):
                    e.wait_ge(gu_done, k * NCH + c + 1 + RING)
                    e.wait_ge(silu_step, 2 * (k * NCH + c) + 1)
                    e.activation(flat(th[:, :, :]), ps[0:F, 1, :], ACT.Tanh, scale=0.5).then_inc(th_ready, 1)
                    if not last:
                        gather_out(c + 1, 1 - p)
                    e.wait_ge(eo_done, k * NCH + c + 1 + RING)
                    e.wait_ge(slots_ready, k * NCH + c + 1)
                    e.wait_ge(combined, CE * (k * NCH + c + 1))
                    for q in range(CE):
                        ins = e.activation(eoh[p][:, q, :], ps[:, 1, q * D:(q + 1) * D], ACT.Copy, scale=wslot[p][:, q:q + 1])
                    ins.then_inc(eoh_ready, 1)

                gather_out(0, 0)
                step(0, 0)
                ring_loop(e, step, 1, NCH - 2)
                step(NCH - 1, 1, last=True)
                e.wait_ge(y_done, k + 1)
                for j in range(NC):
                    e.activation(yT[:, j * BANK:(j + 1) * BANK], ps[:, 4 + j, :], ACT.Copy).then_inc(yT_ready, 1)

            e.wait_ge(gate_turned, 1)
            e.activation(gateT[:, :], ps[:, 2, 0:E], ACT.Copy).then_inc(gate_copied, 1)
            transposed(0)
            exps(0)
            def copy_weights(c, p):
                e.wait_ge(w_turned, c + 1 + RING)
                e.activation(gus[p][:, :, :, :].rearrange("p (g e) s f -> p g (e s f)", g=2), ps[:, 4:6, 0:CE * F], ACT.Copy).then_inc(w_copied, 1)
                e.activation(flat(dns[p][:, :, :]), ps[0:F, 6, :], ACT.Copy).then_inc(w_copied, 1)

            copy_weights(0, 0)
            copy_weights(1, 1)
            with e.Fori(1, NCH // RING) as i:
                for p in range(RING):
                    e.wait_ge(w_stored[p], 32 * i)
                    copy_weights(i * RING + p, p)
            experts(0)
            transposed(1)
            for c in range(NC):
                e.wait_ge(ckv_done, c + 1)
                e.activation(ckvT[:, c * BANK:(c + 1) * BANK], ps[:, c % RING, :], ACT.Copy).then_inc(ckvT_ready, 1)
            for u in range(2 * NC):
                r = u % RING
                side, c = u // NC, u % NC
                e.wait_ge(nope_done, u + 1)
                if u >= RING:
                    e.wait_ge(nope_stored[r], 48 * (u // RING))
                e.activation(nh[r][:, :], ps[:, 2 + r, :], ACT.Copy).then_inc(nh_ready, 1)
                e.wait_ge(rsum_ready, u + 1)
                dst = (Kst if side == 0 else Qst)[0][0][0:ROPE3, c * BANK:(c + 1) * BANK]
                e.activation(dst, ra[r][:, :], ACT.Copy).then_inc(hi_ready, 1)
            def pair_step(pair):
                for n, (j, kt) in enumerate(STEPS):
                    lo = max(0, kt * P - j * BANK)
                    for b in range(B):
                        e.wait_ge(scores_done, (pair + 2) * 2 * NS + 2 * n + b + 1)
                        if b == 0:
                            e.wait_ge(pv_done, (pair + 2) * NS + n + 1 - RING)
                        e.activation(probs[n % RING][:, 2 * b:2 * b + 2, lo:BANK], ps[:, 2 * b:2 * b + 2, lo:BANK],
                                     ACT.Exp, scale=SCALE).then_inc(probs_ready, 1)

            with e.Fori(0, NPAIR // RING) as i:
                for p in range(RING):
                    pair_step(i * RING + p)
            transposed(2, norm=False)
            transposed(3)
            exps(1)
            experts(1)

        @blk.vector
        def _(e):
            e.sem_inc(added, RING)

            def layernorm(n):
                for t in range(NT):
                    if n == 0 and t % TG == 0:
                        e.wait_ge(x_in_s, 64)
                    e.bn_stats(stats[:, t, :], x[:, t, :]).then_inc(stat_done, 1)
                e.wait_ge(stat_done, NT * (n + 1))
                for t in range(NT):
                    e.bn_aggr(mv[:, t, :], stats[:, t, :]).then_inc(moments, 1)
                e.wait_ge(moments, NT * (n + 1))
                e.tensor_scalar(var[:, :], mv[:, :, 1], EPS, None, ALU.add).then_inc(var_ready, 1)
                e.wait_ge(sd_ready, n + 1)
                e.reciprocal(rstd[:, :], sd[:, :]).then_inc(rstd_ready, 1)
                e.wait_ge(rstd_ready, n + 1)
                if n >= 1:
                    e.wait_ge(split_done, NG)
                for t in range(NT):
                    e.tensor_scalar(xn[:, t, :], x[:, t, :], mv[:, t, 0:1], rstd[:, t:t + 1],
                                    ALU.subtract, ALU.mult).then_inc(xn_ready, 1)

            def route(k):
                s0 = 5 * k
                lg = ps[:, 2, :].rearrange("p (t e) -> p t e", t=NT)
                pos = ps[:, 3, :].rearrange("p (t e) -> p t e", t=NT)

                def wide_of(a):
                    return a[:, :].unsqueeze(2).broadcast_to([P, NT, E])

                e.wait_ge(logits_done, k + 1)
                e.tensor_reduce(top[:, :], lg, AX.X, ALU.max).then_inc(soft, 1)
                e.wait_ge(soft, s0 + 1)
                e.tensor_tensor(zl[:, :, :], lg, wide_of(top), ALU.subtract).then_inc(soft, 1)
                e.wait_ge(exp_done, k + 1)
                e.tensor_reduce(den[:, :], zl[:, :, :], AX.X, ALU.add).then_inc(soft, 1)
                e.wait_ge(soft, s0 + 3)
                e.reciprocal(rden[:, :], den[:, :]).then_inc(soft, 1)
                e.wait_ge(soft, s0 + 4)
                e.tensor_tensor(pr[:, :, :], zl[:, :, :], wide_of(rden), ALU.mult).then_inc(soft, 1)
                e.wait_ge(soft, s0 + 5)
                for t in range(NT):
                    e.max(t8[:, t, :], pr[:, t, :]).then_inc(top8, 1)
                e.wait_ge(top8, NT * (k + 1))
                for t in range(NT):
                    e.match_replace(rep[:, t, :], t8[:, t, :], pr[:, t, :], -1.0).then_inc(replaced, 1)
                e.wait_ge(replaced, NT * (k + 1))
                q0 = 8 * k
                e.tensor_scalar(maskb[:, :, :], rep[:, :, :], 0.0, None, ALU.is_lt).then_inc(routed, 1)
                e.tensor_reduce(den[:, :], t8[:, :, :], AX.X, ALU.add).then_inc(routed, 1)
                e.wait_ge(routed, q0 + 2)
                e.reciprocal(rden[:, :], den[:, :]).then_inc(routed, 1)
                e.tensor_tensor(wr[:, :, :], pr[:, :, :], maskb[:, :, :], ALU.mult).then_inc(routed, 1)
                e.tensor_scalar(zl[:, :, :], rep[:, :, :], 0.0, UNROUTED, ALU.is_ge, ALU.mult).then_inc(posm_ready, 1)
                e.wait_ge(posm_ready, 2 * k + 1)
                e.wait_ge(pos_done, k + 1)
                e.tensor_tensor(posm[:, :, :], pos, zl[:, :, :], ALU.add).then_inc(posm_ready, 1)
                a0 = 3 * k
                e.tensor_reduce(least[:, :], pos[0:1], AX.X, ALU.min).then_inc(act_step, 1)
                e.wait_ge(act_step, a0 + 1)
                e.tensor_scalar(least[:, :], least[:, :], float(CAP), None, ALU.is_lt).then_inc(act_step, 1)
                e.wait_ge(act_step, a0 + 2)
                e.tensor_reduce(nactf[:, :], least[:, :], AX.X, ALU.add).then_inc(act_step, 1)
                e.wait_ge(act_step, a0 + 3)
                e.tensor_copy(nact[:, :], nactf[:, :]).then_inc(nact_ready, 1)
                e.wait_ge(routed, q0 + 4)
                e.scalar_tensor_tensor(out=pr[:, :, :], in0=wr[:, :, :], scalar=0.25, in1=wide_of(rden), op0=ALU.mult, op1=ALU.mult).then_inc(routed, 1)
                e.wait_ge(routed, q0 + 5)
                e.wait_ge(info_const, 2 * (k + 1))
                e.tensor_copy(info[:, :, :, 2], pr[:, :, :]).then_inc(routed, 1)
                e.wait_ge(routed, q0 + 6)
                e.tensor_tensor(wr[:, :, :], pr[:, :, :], info[:, :, :, 2], ALU.subtract).then_inc(routed, 1)
                e.wait_ge(routed, q0 + 7)
                e.tensor_copy(info[:, :, :, 3], wr[:, :, :]).then_inc(routed, 1)
                e.wait_ge(routed, q0 + 8)
                e.tensor_tensor(info[:, :, :, 4], wr[:, :, :], info[:, :, :, 3], ALU.subtract).then_inc(onehot_ready[k], 1)
                e.wait_ge(nact_ready, k + 1)
                e.wait_ge(posm_ready, 2 * k + 2)

            def experts(k):
                n = e.value_load(nact[0:1, 0:1], min_val=4, max_val=NT)

                def onehots(c):
                    with e.Fori(0, n) as t:
                        for q in range(CE):
                            ins = e.tensor_scalar(onehot[:, bass.ds(t, 1), q, :].rearrange("p o c -> p (o c)"), iotab[:, :],
                                                  posm[:, bass.ds(t, 1), bass.ds(c * CE + q, 1)].rearrange("p a b -> p (a b)"),
                                                  None, ALU.is_equal)
                        ins.then_inc(onehot_ready[k], 1)

                def slots(c, p):
                    u = k * NCH + c
                    e.wait_ge(gathered, u + 1)
                    e.tensor_copy(idx[:, :, 0:5], ps[:, 3, 0:CE * 8].rearrange("p (e w) -> p e w", w=8)[:, :, 0:5]).then_inc(idx_ready, 1)
                    e.wait_ge(idx_ready, u + 2)
                    e.scalar_tensor_tensor(out=tok[p][:, :], in0=idx[:, :, 1], scalar=float(P), in1=idx[:, :, 0],
                                           op0=ALU.mult, op1=ALU.add).then_inc(slot_step, 1)
                    e.tensor_tensor(wtmp[:, :], idx[:, :, 2], idx[:, :, 3], ALU.add).then_inc(slot_step, 1)
                    e.wait_ge(slot_step, 2 * u + 2)
                    e.tensor_tensor(wslot[p][:, :], wtmp[:, :], idx[:, :, 4], ALU.add).then_inc(slots_ready, 1)

                def step(c, p, h=0, ahead=2):
                    u = k * NCH + c
                    e.wait_ge(th_ready, u + 1)
                    e.scalar_tensor_tensor(out=flat(ga[:, :, :]), in0=flat(th[:, :, :]), scalar=1.0, in1=ps[0:F, 1, :],
                                           op0=ALU.add, op1=ALU.mult).then_inc(silu_step, 1)
                    e.wait_ge(silu_step, 2 * u + 2)
                    e.tensor_tensor(flat(hT[:, :, :]), flat(ga[:, :, :]), ps[0:F, 2, :], ALU.mult).then_inc(silu_step, 1)
                    if ahead >= 1:
                        slots(c + 1, 1 - p)
                    e.wait_ge(eoh_ready, u + 1)
                    for q in range(CE):
                        ins = e.scalar_tensor_tensor(out=eol[p][:, q, :], in0=ps[:, 1, q * D:(q + 1) * D], scalar=wslot[p][:, q:q + 1],
                                                     in1=eoh[p][:, q, :], op0=ALU.mult, op1=ALU.subtract)
                    ins.then_inc(eol_ready, 1)
                    if ahead >= 2:
                        onehots(c + 2)
                    for q in range(CE):
                        e.wait_ge(combined, (u + 1) * CE + q + 1)
                        e.tensor_scalar(place[q][:, 0:NEAR], iota_s[:, 0:NEAR], tok[p][:, q:q + 1], None, ALU.is_equal).then_inc(placed, 1)
                        with e.If(n > NEAR // P):
                            e.tensor_scalar(place[q][:, NEAR:N], iota_s[:, NEAR:N], tok[p][:, q:q + 1], None, ALU.is_equal).then_inc(placed_far[k], 1)

                onehots(0)
                slots(0, 0)
                onehots(1)
                step(0, 0)
                ring_loop(e, step, 1, NCH - 4)
                step(NCH - 3, 1)
                step(NCH - 2, 0, ahead=1)
                step(NCH - 1, 1, ahead=0)

            def add_to_x(n):
                for g in range(NG):
                    if n == 1:
                        e.wait_ge(wo_done, g + 1)
                        bank = 2 + g % RING
                    else:
                        e.wait_ge(y_turned, (n // 2) * NG + g + 1)
                        bank = g % RING
                    t = slice(g * TG, (g + 1) * TG)
                    e.tensor_tensor(x[:, t, :], x[:, t, :], ps[:, bank, :].rearrange("p (t d) -> p t d", d=D), ALU.add).then_inc(added, 1)
                e.wait_ge(added, NG * (n + 1) + RING)

            e.wait_ge(bf_consts, 5)
            layernorm(0)
            route(0)
            experts(0)
            add_to_x(0)
            layernorm(1)

            e.wait_ge(cs_in, 32)
            for u in range(2 * NC + 1):
                if u < 2 * NC:
                    side, c, r = u // NC, u % NC, u % RING
                    cols = slice(c % (T // BANK) * BANK, (c % (T // BANK) + 1) * BANK)
                    e.wait_ge(rope_done, u + 1)
                    if u >= RING:
                        e.wait_ge(lo_ready, u - RING + 1)
                    e.tensor_tensor(ra[r][:, :], ps[0:ROPE3, 4 + 2 * r, :], cs[:, 0, cols], ALU.mult).then_inc(ra_ready, 1)
                    e.tensor_tensor(rb[r][:, :], ps[0:ROPE3, 5 + 2 * r, :], cs[:, 1, cols], ALU.mult).then_inc(rb_ready, 1)
                    e.wait_ge(nh_ready, u + 1)
                    e.tensor_tensor(nl[r][:, :], ps[:, 2 + r, :], nh[r][:, :], ALU.subtract).then_inc(nl_ready, 1)
                if u >= 1:
                    v = u - 1
                    side, c, r = v // NC, v % NC, v % RING
                    dst = (Kst if side == 0 else Qst)[0][0][:, c * BANK:(c + 1) * BANK]
                    low = slice(DR, 2 * DR) if side == 0 else slice(2 * DR, 3 * DR)
                    e.wait_ge(hi_ready, v + 1)
                    e.tensor_tensor(dst[low], ra[r][low, :], dst[low], ALU.subtract).then_inc(lo_ready, 1)
            for g in range(NG):
                e.wait_ge(v_done, g + 1)
                e.tensor_copy(V[:, TG * g:TG * (g + 1), :, :].rearrange("p a b c -> p (a b c)"), ps[:, 6 + g % RING, :]).then_inc(v_ready, 1)

            def maxima(pair, first, last):
                for m in range(first, last):
                    jt, o, q = UNITS[m]
                    b, h = q // 2, q % 2
                    w = min(BANK, (jt + 1) * P - o)
                    col = h * NT + b * TB + jt
                    e.wait_ge(mscores_done, pair * NU + m + 1)
                    e.tensor_reduce(mxh[:, o // BANK, col:col + 1], ps[:, 6 + m % RING, 0:w], AX.X, ALU.max).then_inc(mx_ready, 1)

            def shifts(pair):
                e.wait_ge(mx_ready, (pair + 1) * NU + RING)
                e.tensor_tensor(mx[:, :], mxh[:, 0, :], mxh[:, 1, :], ALU.max).then_inc(mx_joined, 1)
                e.wait_ge(mx_turned, pair + 2)
                e.tensor_scalar(shf[:, :], ps[0:2 * NT, 7, 0:P], -1.0, None, ALU.mult).then_inc(shf_ready, 1)

            def copy_values(pair, j):
                done = sum(1 for (jj, _) in STEPS if jj <= j)
                e.wait_ge(pv_done, (pair + 2) * NS + done)
                e.tensor_copy(oS[j][:, :], ps[:, 4 + j, :]).then_inc(oS_ready, 1)

            def normalise(pair, j):
                u = pair * 2 + j
                e.wait_ge(o_turned, u + 1)
                o = ps[:, 6, :].rearrange("p (t s c) -> p t s c", t=4, s=4)
                e.reciprocal(ord_[:, :, :], o[:, :, :, HD]).then_inc(oden_ready, 1)
                e.wait_ge(oden_ready, u + 1)
                for b in range(B):
                    dst = attn[:, b * TB + 4 * j:b * TB + 4 * j + 4, bass.ds(pair * 2 * HD, 2 * HD)].rearrange("p t (h c) -> p t h c", h=2)
                    ins = e.tensor_tensor(dst, o[:, :, 2 * b:2 * b + 2, 0:HD],
                                          ord_[:, :, 2 * b:2 * b + 2].unsqueeze(3).broadcast_to([P, 4, 2, HD]), ALU.mult)
                ins.then_inc(attn_ready, 1)

            def pair_step(pair, p=0, h=0, first=False, last=False):
                early = US * (BANK // P - U0)
                if not first:
                    normalise(pair - 1, 1)
                if not last:
                    maxima(pair + 1, 0, early)
                copy_values(pair, 0)
                if not last:
                    maxima(pair + 1, early, NU)
                    e.wait_ge(shift_in[p], 32 * (h + 1))
                    shifts(pair + 1)
                normalise(pair, 0)
                copy_values(pair, 1)

            e.wait_ge(mx_const, 1)
            maxima(0, 0, NU)
            shifts(0)
            pair_step(0, first=True)
            ring_loop(e, pair_step, 1, NPAIR - 2)
            pair_step(NPAIR - 1, last=True)
            normalise(NPAIR - 1, 1)
            add_to_x(1)
            layernorm(2)
            route(1)
            experts(1)
            add_to_x(2)

        @blk.tensor
        def _(e):
            e.sem_inc(w_turned, RING)
            e.sem_inc(gu_done, RING)
            e.sem_inc(eo_done, RING)
            e.sem_inc(combined, 2 * CE)
            e.sem_inc(mx_ready, RING)
            e.sem_inc(probs_ready, RING)
            e.sem_inc(pv_done, 2 * NS)
            e.sem_inc(scores_done, 4 * NS)
            e.sem_inc(oS_ready, 2)

            def transposes(n, src):
                for g in range(NG):
                    if n != 2:
                        e.wait_ge(xn_ready, (n - n // 3) * NT + (g + 1) * TG)
                    e.wait_ge(xnT_ready, n * NG + g + 1)
                    for q in range(TG):
                        ins = e.transpose(ps[:, g % RING, q * P:(q + 1) * P], src[:, g * TG + q, :], ident)
                    ins.then_inc(turned, 1)

            def logits():
                for t in range(NT):
                    if t % TG == 0:
                        e.wait_ge(xnT_ready, (0 if logits.k == 0 else 3 * NG) + t // TG + 1 + RING)
                    ins = e.matmul(ps[:, 2, t * E:(t + 1) * E], xnT[:, t * P:(t + 1) * P], gateT[:, :], start=True, stop=True)
                ins.then_inc(logits_done, 1)
                logits.k += 1
            logits.k = 0

            def turn_weights():
                with e.Fori(0, NCH // RING) as i:
                    for p in range(RING):
                        c = i * RING + p
                        e.wait_ge(nat_in[p], 32 * (i + 1))
                        e.wait_ge(w_copied, 2 * c + 1)
                        for q in range(2 * CE):
                            e.transpose(ps[:, 4 + q // CE, (q % CE) * F:(q % CE + 1) * F], wgn[p][:, q, :], ident[0:F, 0:F])
                        for q in range(CE):
                            ins = e.transpose(ps[0:F, 6, q * D:(q + 1) * D], wdn[p][:, q, :], ident)
                        ins.then_inc(w_turned, 1)

            def positions(k):
                e.wait_ge(routed, 8 * k + 1)
                e.matmul(ps[:, 3, :], zerosb[:, 0:P], zerosb[:, :], start=True, stop=False, skip_group_check=True)
                for t in range(NT - 1):
                    o = ps[:, 3, (t + 1) * E:].rearrange("p (t e) -> p t e", e=E)
                    e.matmul(o, onesb[:, :], maskb[:, t:t + 1, :].broadcast_to([P, NT - 1 - t, E]),
                             start=False, stop=False, skip_group_check=True)
                e.matmul(ps[:, 3, :], beforeb[:, :], flat(maskb[:, :, :]), start=False, stop=True, skip_group_check=True).then_inc(pos_done, 1)

            def experts(k):
                e.wait_ge(nact_ready, k + 1)
                n = e.value_load(nact[0:1, 0:1], min_val=4, max_val=NT)
                e.wait_ge(split_done, NG * (k + 1))
                for j in range(NC):
                    e.matmul(ps[:, 4 + j, :], zerosb[:, 0:P], zerosb[:, :], start=True, stop=False, skip_group_check=True)

                def gather(c, p):
                    u = k * NCH + c
                    e.wait_ge(bufT_ready, u + 1)
                    e.wait_ge(idx_ready, u + 1)

                    def tile(t, first=False, last=False):
                        e.wait_ge(onehot_ready[k], c * n + t + 2)
                        for part in range(3):
                            e.matmul(ps[:, 0, :], xp[:, bass.ds(t, 1), part, :].rearrange("p o d -> p (o d)"),
                                     onehot[:, bass.ds(t, 1), :, :].rearrange("p o e c -> p (o e c)"),
                                     start=first and part == 0, stop=last and part == 2, skip_group_check=True)
                        for q in range(CE):
                            ins = e.matmul(ps[:, 3, q * 8:q * 8 + 5], onehot[:, bass.ds(t, 1), q, :].rearrange("p o c -> p (o c)"),
                                           info[:, bass.ds(t, 1), bass.ds(c * CE + q, 1), :].rearrange("p a b w -> p (a b w)"),
                                           start=first and q == 0, stop=last, skip_group_check=True)
                        if last:
                            ins.then_inc(gathered, 1)

                    tile(0, first=True)
                    with e.Fori(1, n - 1) as t:
                        tile(t)
                    tile(n - 1, last=True)

                def combine(c, p):
                    u = k * NCH + c
                    e.wait_ge(eoh_ready, u + 1)
                    e.wait_ge(eol_ready, u + 2)
                    for q in range(CE):
                        e.wait_ge(placed, u * CE + q + 1)
                        with e.If(n > NEAR // P):
                            e.wait_ge(placed_far[k], c * CE + q + 1)
                            for w in (eoh, eol):
                                for o, m in ((NEAR, 256), (2 * BANK, BANK), (3 * BANK, BANK)):
                                    e.matmul(ps[:, 4 + o // BANK, o % BANK:o % BANK + m], w[p][:, q, :], place[q][:, o:o + m],
                                             start=False, stop=False, skip_group_check=True)
                        for w in (eoh, eol):
                            for o, m in ((0, BANK), (BANK, 256)):
                                ins = e.matmul(ps[:, 4 + o // BANK, 0:m], w[p][:, q, :], place[q][:, o:o + m],
                                               start=False, stop=False, skip_group_check=True)
                        ins.then_inc(combined, 1)

                def step(c, p, h, first=False, last=False):
                    u = k * NCH + c
                    e.wait_ge(bufT_ready, u + 2)
                    e.wait_ge(gus_in[p], 16 * (k * NCH // RING + h + 1))
                    e.wait_ge(eol_ready, u + 1)
                    for half, bank in ((0, 1), (1, 2)):
                        for q in range(CE):
                            ins = e.matmul(ps[0:F, bank, q * CAP:(q + 1) * CAP], gus[p][:, q, half, :], bufT[p][:, q, :], start=True, stop=True)
                    ins.then_inc(gu_done, 1)
                    if not last:
                        gather(c + 1, 1 - p)
                    e.wait_ge(silu_step, 2 * u + 3)
                    e.wait_ge(dns_in[p], 16 * (k * NCH // RING + h + 1))
                    for q in range(CE):
                        ins = e.matmul(ps[:, 1, q * D:(q + 1) * D], hT[:, q, :], dns[p][:, q, :], start=True, stop=True)
                    ins.then_inc(eo_done, 1)
                    if not first:
                        combine(c - 1, 1 - p)

                gather(0, 0)
                step(0, 0, 0, first=True)
                ring_loop(e, step, 1, NCH - 2)
                step(NCH - 1, 1, (NCH - 1) // RING, last=True)
                combine(NCH - 1, 1)
                for j in range(NC):
                    ins = e.matmul(ps[:, 4 + j, :], zerosb[:, 0:P], zerosb[:, :], start=False, stop=True, skip_group_check=True)
                ins.then_inc(y_done, 1)
                for g in range(NG):
                    e.wait_ge(yT_ready, k * NC + g + 1)
                    e.wait_ge(added, 2 * k * NG + g + 1)
                    for q in range(TG):
                        t = g * TG + q
                        ins = e.transpose(ps[:, g % RING, q * D:(q + 1) * D], yT[:, t * P:(t + 1) * P], ident)
                    ins.then_inc(y_turned, 1)

            e.wait_ge(consts_in, 48)
            e.wait_ge(gate_in, 16)
            e.transpose(ps[:, 2, 0:E], gate_n[:, :], ident[0:E, 0:E]).then_inc(gate_turned, 1)
            e.wait_ge(bf_consts, 5)
            e.wait_ge(memsets, 2)
            e.wait_ge(gate_copied, 1)
            transposes(0, xn)
            logits()
            turn_weights()
            positions(0)
            e.wait_ge(w_copied, 2 * NCH + 1)
            experts(0)
            transposes(1, xn)

            e.wait_ge(watt_in, 16 * 7)
            for c in range(NC):
                e.wait_ge(xnT_ready, NG + c + 1 + RING)
                if c >= RING:
                    e.wait_ge(ckvT_ready, c - 1)
                else:
                    e.wait_ge(xnT_ready, 2 * NG + RING)
                e.matmul(ps[:, c % RING, :], wat[:, 0, :], xnT[:, c * BANK:(c + 1) * BANK], start=True, stop=True).then_inc(ckv_done, 1)
            e.wait_ge(ckvT_ready, NC)
            e.wait_ge(rope_weights, 6)

            for u in range(2 * NC):
                side, c, r = u // NC, u % NC, u % RING
                src, w = ((ckvT, 1), (xnT, 3))[side]
                cols = slice(c * BANK, (c + 1) * BANK)
                if u >= RING:
                    e.wait_ge(nl_ready, u - 1)
                    e.wait_ge(rb_ready, u - 1)
                e.matmul(ps[:, 2 + r, :], wat[:, w, :], src[:, cols], start=True, stop=True).then_inc(nope_done, 1)
                for v in range(2):
                    ins = e.matmul(ps[0:ROPE3, 4 + 2 * r + v, :], wrep[:, side, v, :, :].rearrange("p r d -> p (r d)"), src[:, cols], start=True, stop=True)
                ins.then_inc(rope_done, 1)
            for g in range(NG):
                if g >= RING:
                    e.wait_ge(v_ready, g - 1)
                elif g == 0:
                    e.wait_ge(rb_ready, 2 * NC)
                for q in range(TG):
                    t = TG * g + q
                    ins = e.matmul(ps[:, 6 + g % RING, q * P:(q + 1) * P], ckvT[:, t * P:(t + 1) * P], wat[:, 2, :], start=True, stop=True)
                ins.then_inc(v_done, 1)

            e.wait_ge(rope_copied, 16 * 6 * NC)
            e.wait_ge(lo_ready, 2 * NC)
            e.wait_ge(nl_ready, 2 * NC)
            e.wait_ge(v_ready, NG)

            def maxima(pair, p, first, last):
                for m in range(first, last):
                    jt, o, q = UNITS[m]
                    b, h = q // 2, q % 2
                    w = min(BANK, (jt + 1) * P - o)
                    diagonal = o + w == (jt + 1) * P
                    e.wait_ge(mx_ready, pair * NU + m + 1)
                    ins = e.matmul(ps[:, 6 + m % RING, 0:w], Qst[p][h][0:ROWS, b * T + jt * P:b * T + (jt + 1) * P],
                                   Kst[p][h][0:ROWS, b * T + o:b * T + o + w], start=True, stop=not diagonal, skip_group_check=True)
                    if diagonal:
                        ins = e.matmul(ps[:, 6 + m % RING, w - P:w], identb[:, :], maskQ[:, :], start=False, stop=True, skip_group_check=True)
                    ins.then_inc(mscores_done, 1)

            def turn_maxima(pair):
                e.wait_ge(mx_joined, pair + 1)
                e.transpose(ps[0:2 * NT, 7, 0:P], mx[:, :], ident).then_inc(mx_turned, 1)

            e.wait_ge(stage_in[0], 64)
            maxima(0, 0, 0, NU)
            turn_maxima(0)

            e.wait_ge(vst_const, 2 * RING)

            def turn(pair, j):
                u = pair * 2 + j
                e.wait_ge(oS_ready, u + 1 + 2)
                e.wait_ge(attn_ready, u + 1)
                for q in range(4):
                    ins = e.transpose(ps[:, 6, q * P:(q + 1) * P], oS[j][:, q * P:(q + 1) * P], ident)
                ins.then_inc(o_turned, 1)

            def pair_step(pair, p, half, first=False, last=False):
                e.wait_ge(stage_in[p], 64 * (half + 1))
                e.wait_ge(shift_in[p], 32 * (half + 1))
                e.wait_ge(vst_ready, pair + 1)

                def scores(n):
                    j, kt = STEPS[n]
                    lo = max(0, kt * P - j * BANK)
                    diagonal = kt * P >= j * BANK
                    for b in range(B):
                        e.wait_ge(probs_ready, pair * 2 * NS + 2 * n + b + 1)
                        for h in range(2):
                            ins = e.matmul(ps[:, 2 * b + h, lo:BANK], Kst[p][h][0:ROWS + 1, b * T + kt * P:b * T + (kt + 1) * P],
                                           Qst[p][h][0:ROWS + 1, b * T + j * BANK + lo:b * T + (j + 1) * BANK],
                                           start=True, stop=not diagonal, skip_group_check=True)
                            if diagonal:
                                ins = e.matmul(ps[:, 2 * b + h, lo:lo + P], identb[:, :], maskT[:, :], start=False, stop=True, skip_group_check=True)
                        ins.then_inc(scores_done, 1)

                def weighted(n):
                    j, kt = STEPS[n]
                    lo = max(0, kt * P - j * BANK)
                    e.wait_ge(probs_ready, pair * 2 * NS + 2 * n + 2 + RING)
                    if kt == 0:
                        e.wait_ge(oS_ready, pair * 2 + j + 1)
                    for q in range(4):
                        b, h = q // 2, q % 2
                        ins = e.matmul(ps[VW * q:VW * (q + 1), 4 + j, lo:BANK], Vst[p][:, b * TB + kt, h, :], probs[n % RING][:, q, lo:BANK],
                                       start=(kt == 0), stop=(kt == (j + 1) * BANK // P - 1), skip_group_check=True)
                    ins.then_inc(pv_done, 1)

                scores(0)
                for n in range(NS):
                    if n + 1 < NS:
                        scores(n + 1)
                    if n == U0 and not last:
                        e.wait_ge(stage_in[1 - p], 64 * (half + p + 1))
                        e.wait_ge(attn_ready, pair * 2 + 1)
                        e.wait_ge(shf_ready, pair + 2)
                    m = (n - U0) * US
                    units = not last and 0 <= m < NU
                    if units:
                        maxima(pair + 1, 1 - p, m, m + US // 2)
                    weighted(n)
                    if units:
                        maxima(pair + 1, 1 - p, m + US // 2, m + US)
                    if n == 1 and not first:
                        turn(pair - 1, 1)
                    if n == NS - 2 and not last:
                        turn_maxima(pair + 1)
                    if n == NS - 1:
                        turn(pair, 0)

            pair_step(0, 0, 0, first=True)
            ring_loop(e, pair_step, 1, NPAIR - 2)
            pair_step(NPAIR - 1, 1, (NPAIR - 1) // RING, last=True)
            turn(NPAIR - 1, 1)

            e.wait_ge(attn_ready, 2 * NPAIR + 1)
            transposes(2, attn)
            for g in range(NG):
                e.wait_ge(xnT_ready, 2 * NG + g + 1 + RING)
                e.wait_ge(added, NG + g + 1)
                for q in range(TG):
                    t = g * TG + q
                    ins = e.matmul(ps[:, 2 + g % RING, q * D:(q + 1) * D], xnT[:, t * P:(t + 1) * P], wat[:, 4, :], start=True, stop=True)
                ins.then_inc(wo_done, 1)
            transposes(3, xn)
            logits()
            positions(1)
            experts(1)


_INS = ['L0_attn_x', 'L0_attn_W_kv_down', 'L0_attn_W_k_up', 'L0_attn_W_v_up', 'L0_attn_W_q', 'L0_attn_W_q_rope',
        'L0_attn_W_k_rope', 'L0_attn_W_o', 'L0_ffn_gate_weight', 'L0_ffn_gate_up_proj', 'L0_ffn_down_proj']


def constants():
    a = np.arange(P)
    before = (a[:, None] < a[None, :]).astype(np.float32)
    masked = np.float32(MASKED)
    squares = np.stack([np.eye(P, dtype=np.float32), before, masked * before.T, masked * before])
    inv_freq = np.float32(1.0) / np.power(np.float32(10000.0), np.arange(0, DR, 2, dtype=np.float32) / np.float32(DR))
    angle = (np.arange(T, dtype=np.float32)[None, :] * inv_freq.astype(np.float32)[:, None]).astype(np.float32)
    c, s = np.cos(angle), np.sin(angle)
    return {
        "squares": squares.astype(np.float32),
        "cos3": np.tile(np.concatenate([c, c]), (3, 1)).astype(np.float32),
        "sin3": np.tile(np.concatenate([-s, s]), (3, 1)).astype(np.float32),
        "iota": np.arange(N, dtype=np.float32)[None, :],
        "tokinfo": np.stack(np.broadcast_arrays(a[:, None], np.arange(NT)[None, :]), -1).astype(np.float32),
    }


def kernel(**inputs):
    from concourse import bacc
    from concourse.bass_utils import run_bass_kernel_spmd

    nc = bacc.Bacc("TRN2", target_bir_lowering=False, num_devices=1)
    arrays, args = {}, []
    given = {n: np.ascontiguousarray(inputs[n]) for n in _INS}
    for name, a in {**given, **constants()}.items():
        arrays[f"in_{name}"] = a
        args.append(nc.dram_tensor(f"in_{name}", a.shape, mybir.dt.from_np(a.dtype), kind="ExternalInput").ap())
    args.append(nc.dram_tensor("out_0", (B, T, D), F32, kind="ExternalOutput").ap())
    build(nc, *args)
    r = run_bass_kernel_spmd(nc, [arrays], core_ids=[0])
    return r.results[0]["out_0"]
```

```python
from contextlib import ExitStack

import numpy as np
import concourse.bass as bass
from concourse import mybir

F32 = mybir.dt.float32
F32R = mybir.dt.float32r
BF16 = mybir.dt.bfloat16
ALU = mybir.AluOpType
ACT = mybir.ActivationFunctionType
AX = mybir.AxisListType

P = 128
B, T, D = 2, 1024, 128
N = B * T
NT = N // P
TB = T // P
NH, HD, DR = 16, 8, 32
E, F, TOPK, CAP = 32, 96, 8, 128
CE = 4
NCH = E // CE
BANK = 512
NPAIR = NH // 2
ROPE3 = 3 * DR
NOPE3 = 3 * HD
ROWS = ROPE3 + NOPE3
VW = 32
SCALE = 1.0 / float(np.sqrt(HD + DR))
EPS = 1e-5
UNROUTED = 4096.0
MASKED = -1e30
NG = 4
TG = NT // NG
LEAST = CAP * E // TOPK // P + 1
NEAR = (LEAST + 1) * P
RING = 2

STEPS = [(0, 0), (0, 1), (1, 0), (0, 2), (1, 1), (0, 3), (1, 2), (1, 3), (1, 7), (1, 6), (1, 5), (1, 4)]
EARLY = max(n for n, (j, i) in enumerate(STEPS) if j == 0 or i < BANK // P)
OPENS = [min(n for n, (jj, _) in enumerate(STEPS) if jj == j) for j in range(T // BANK)]
CLOSES = [max(n for n, (jj, _) in enumerate(STEPS) if jj == j) for j in range(T // BANK)]
NS = len(STEPS)
UNITS = []
for jt in range(TB):
    for o in range(0, (jt + 1) * P, BANK):
        w = min(BANK, (jt + 1) * P - o)
        nq = BANK // w if BANK % w == 0 else 1
        UNITS += [(jt, o, w, q, nq) for q in range(0, 4, nq)]
EARLYU = sum(1 for u in UNITS if u[0] < BANK // P)
NU = len(UNITS)
SHARE = [4, 4, 5, 4, 5, 4, 5, 4, 3, 0, 0, 0]
FIRSTU = min(n for n in range(NS) if SHARE[n])
LASTU = max(n for n in range(NS) if SHARE[n])
BEFORE = [sum(SHARE[:n]) for n in range(NS + 1)]
NC = N // BANK


def build(nc, x_in, w_kv_down, w_k_up, w_v_up, w_q, w_q_rope, w_k_rope, w_o,
          gate_weight, gate_up_proj, down_proj, squares, cos3, sin3, iota, tokinfo, out):
    ctx = ExitStack()

    def sb(name, shape, dt=F32, stack=None):
        return (stack or ctx).enter_context(nc.sbuf_tensor(name, shape, dt))

    def sem(name):
        return ctx.enter_context(nc.semaphore(name))

    def flat(a):
        return a.rearrange("p a b -> p (a b)")

    def flat3(a):
        return a.rearrange("p a b c -> p (a b c)")

    def raw(a):
        return a.bitcast(F32)

    with ctx:
        guT_d = nc.dram_tensor("guT_d", [NCH, P, CE * 2 * F], F32).ap()
        dnT_d = nc.dram_tensor("dnT_d", [NCH, F, CE * D], F32).ap()
        kn_d = nc.dram_tensor("kn_d", [3, NH * HD, N], F32).ap()
        qn_d = nc.dram_tensor("qn_d", [3, NH * HD, N], F32).ap()

        x = sb("x", [P, NT, D])
        xn = sb("xn", [P, NT, D])
        xnT = sb("xnT", [D, N])
        sq = sb("sq", [P, 4, P])
        ident = sq[:, 0, :]
        identb = sb("identb", [P, P], BF16)
        beforeb = sb("beforeb", [P, P], BF16)
        maskT = sb("maskT", [P, P], BF16)
        maskQw = sb("maskQw", [P, 2 * P], BF16)
        maskQ = maskQw[:, P:2 * P]
        onesb = sb("onesb", [P, P], BF16)
        zerosb = sb("zerosb", [P, BANK], BF16)
        gate_n = sb("gate_n", [E, D])
        gateT = sb("gateT", [D, E])
        iota_s = sb("iota_s", [P, N])
        iotab = sb("iotab", [P, P], BF16)
        tokinfo_s = sb("tokinfo_s", [P, NT, 2])
        stats = sb("stats", [P, NT, 6])
        mv = sb("mv", [P, NT, 2])
        var = sb("var", [P, NT])
        sd = sb("sd", [P, NT])
        rstd = sb("rstd", [P, NT])
        wat = sb("wat", [P, 5, D])
        wrope = sb("wrope", [P, 2, DR])
        wrep = sb("wrep", [P, 2, 2, 3, DR])
        gus = [sb(f"gus{p}", [P, CE, 2, F]) for p in range(RING)]
        dns = [sb(f"dns{p}", [F, CE, D]) for p in range(RING)]

        moe = ExitStack()
        wgn = [sb(f"wgn{p}", [F, CE * 2, D], F32, moe) for p in range(RING)]
        wdn = [sb(f"wdn{p}", [D, CE, F], F32, moe) for p in range(RING)]
        xp = sb("xp", [P, NT, 3, D], BF16, moe)
        rem = [sb(f"rem{g}", [P, TG, D], F32, moe) for g in range(NG)]
        top = sb("top", [P, NT], F32, moe)
        zl = sb("zl", [P, NT, E], F32, moe)
        pr = sb("pr", [P, NT, E], F32, moe)
        den = sb("den", [P, NT], F32, moe)
        rden = sb("rden", [P, NT], F32, moe)
        t8 = sb("t8", [P, NT, TOPK], F32, moe)
        rep = sb("rep", [P, NT, E], F32, moe)
        maskb = sb("maskb", [P, NT, E], BF16, moe)
        wr = sb("wr", [P, NT, E], F32, moe)
        info = sb("info", [P, NT, E, 5], BF16, moe)
        posm = sb("posm", [P, NT, E], F32, moe)
        least = sb("least", [1, NT], F32, moe)
        nactf = sb("nactf", [1, 1], F32, moe)
        nact = sb("nact", [1, 1], mybir.dt.int32, moe)
        onehot = sb("onehot", [P, NT, CE, CAP], BF16, moe)
        bufT = [sb(f"bufT{p}", [D, CE, CAP], F32, moe) for p in range(RING)]
        idx = sb("idx", [P, CE, 8], F32, moe)
        tok = [sb(f"tok{p}", [P, CE], F32, moe) for p in range(RING)]
        wslot = [sb(f"wslot{p}", [P, CE], F32, moe) for p in range(RING)]
        wtmp = sb("wtmp", [P, CE], F32, moe)
        th = sb("th", [F, CE, CAP], F32, moe)
        ga = sb("ga", [F, CE, CAP], F32, moe)
        hT = sb("hT", [F, CE, CAP], F32, moe)
        eoh = [sb(f"eoh{p}", [P, CE, D], F32R, moe) for p in range(RING)]
        eol = [sb(f"eol{p}", [P, CE, D], F32R, moe) for p in range(RING)]
        place = [sb(f"place{q}", [P, N], F32R, moe) for q in range(CE)]
        yT = sb("yT", [D, N], F32, moe)
        moe.close()

        att = ExitStack()
        ckvT = sb("ckvT", [D, N], F32, att)
        cs = sb("cs", [ROPE3, 2, T], F32, att)
        ra = [sb(f"ra{p}", [ROPE3, BANK], F32, att) for p in range(RING)]
        rb = [sb(f"rb{p}", [ROPE3, BANK], F32, att) for p in range(RING)]
        nh = [sb(f"nh{p}", [P, BANK], F32R, att) for p in range(RING)]
        nl = [sb(f"nl{p}", [P, BANK], F32R, att) for p in range(RING)]
        V = sb("V", [P, NT, NH, HD], F32, att)
        Vst = [sb(f"Vst{p}", [P, NT, 2, VW], F32, att) for p in range(RING)]
        Kst = [[sb(f"Kst{p}{h}", [P, N], F32R, att) for h in range(2)] for p in range(RING)]
        Qst = [[sb(f"Qst{p}{h}", [P, N], F32R, att) for h in range(2)] for p in range(RING)]
        probs = [sb(f"probs{p}", [P, 4, BANK], F32, att) for p in range(RING)]
        mxh = sb("mxh", [P, 2, 2 * NT], F32, att)
        mx = sb("mx", [P, 2 * NT], F32, att)
        shf = sb("shf", [2 * NT, P], F32R, att)
        oS = [sb(f"oS{j}", [P, BANK], F32, att) for j in range(2)]
        ord_ = sb("ord", [P, 4, 4], F32, att)
        att.close()
        attn = xn

        ps = ctx.enter_context(nc.psum_tensor("ps", [P, 8, BANK], F32))

        x_in_s = [sem(f"x_in_s{g}") for g in range(NG)]
        gate_in, consts_in, iota_in, watt_in, cs_in = (sem(n) for n in ("gate_in", "consts_in", "iota_in", "watt_in", "cs_in"))
        bf_consts, memsets, rope_weights = (sem(n) for n in ("bf_consts", "memsets", "rope_weights"))
        gate_turned, gate_copied = sem("gate_turned"), sem("gate_copied")
        nat_in = [sem(f"nat_in{p}") for p in range(RING)]
        gu_turned, w_turned, w_copied = sem("gu_turned"), sem("w_turned"), sem("w_copied")
        w_stored = [sem(f"w_stored{p}") for p in range(RING)]
        gus_in = [sem(f"gus_in{p}") for p in range(RING)]
        dns_in = [sem(f"dns_in{p}") for p in range(RING)]
        stat_done, moments, var_ready, sd_ready, rstd_ready, xn_ready = (
            sem(n) for n in ("stat_done", "moments", "var_ready", "sd_ready", "rstd_ready", "xn_ready"))
        turned, xnT_ready, logits_done = sem("turned"), sem("xnT_ready"), sem("logits_done")
        part0, rem1, part1, split_done = sem("part0"), sem("rem1"), sem("part1"), sem("split_done")
        soft, exp_done, top8, replaced, routed, info_const, pos_done, posm_ready, act_step, nact_ready = (
            sem(n) for n in ("soft", "exp_done", "top8", "replaced", "routed", "info_const", "pos_done", "posm_ready",
                             "act_step", "nact_ready"))
        onehot_ready = [sem(f"onehot_ready{k}") for k in range(2)]
        placed_far = [sem(f"placed_far{k}") for k in range(2)]
        gathered, bufT_ready, idx_ready, slot_step, slots_ready, gu_done, th_ready, silu_step, eo_done, eoh_ready, eol_ready = (
            sem(n) for n in ("gathered", "bufT_ready", "idx_ready", "slot_step", "slots_ready", "gu_done", "th_ready",
                             "silu_step", "eo_done", "eoh_ready", "eol_ready"))
        placed, combined, y_done, yT_ready, y_turned, added = (
            sem(n) for n in ("placed", "combined", "y_done", "yT_ready", "y_turned", "added"))
        ckv_done, ckvT_ready, nope_done, nh_ready, nl_ready = (
            sem(n) for n in ("ckv_done", "ckvT_ready", "nope_done", "nh_ready", "nl_ready"))
        nope_stored = [sem(f"nope_stored{p}") for p in range(RING)]
        rope_done, ra_ready, rb_ready, rsum_ready, hi_ready, lo_ready = (
            sem(n) for n in ("rope_done", "ra_ready", "rb_ready", "rsum_ready", "hi_ready", "lo_ready"))
        rope_copied, v_done, v_ready, vst_const, vst_ready, rows_const = (
            sem(n) for n in ("rope_copied", "v_done", "v_ready", "vst_const", "vst_ready", "rows_const"))
        stage_in = [[sem(f"stage_in{part}{p}") for p in range(RING)] for part in range(2)]
        shift_in = [sem(f"shift_in{p}") for p in range(RING)]
        mscores_done, mx_const, mx_ready, mx_joined, mx_turned, shf_ready = (
            sem(n) for n in ("mscores_done", "mx_const", "mx_ready", "mx_joined", "mx_turned", "shf_ready"))
        scores_done, probs_ready, pv_done, oS_ready, o_turned, oden_ready, attn_ready, wo_done, out_s = (
            sem(n) for n in ("scores_done", "probs_ready", "pv_done", "oS_ready", "o_turned", "oden_ready", "attn_ready",
                             "wo_done", "out_s"))

        blk = ctx.enter_context(nc.Block())

        def ring_loop(e, step, first, last):
            with e.Fori(0, (last - first + 1) // RING) as i:
                for q in range(RING):
                    step(i * RING + (first + q), (first + q) % RING, i + (first + q) // RING)

        @blk.sync
        def _(e):
            for g in range(NG):
                b, r = g * TG // TB, g * TG % TB
                e.dma_start(x[:, g * TG:(g + 1) * TG, :], x_in[b, r * P:(r + TG) * P].rearrange("(t p) d -> p t d", p=P)).then_inc(x_in_s[g], 16)
            e.dma_start(gate_n[:, :], gate_weight).then_inc(gate_in, 16)

            def load_weights(s, c, p):
                e.wait_ge(w_turned, s + 1)
                e.dma_start(wgn[p][:, :, :], gate_up_proj[bass.ds(c * CE, CE)].rearrange("e (s f) h -> f (e s) h", s=2)).then_inc(nat_in[p], 16)
                e.dma_start(wdn[p][:, :, :], down_proj[bass.ds(c * CE, CE)].rearrange("e h f -> h e f")).then_inc(nat_in[p], 16)

            def store_weights(s, c, p):
                e.wait_ge(w_copied, 2 * s + 4)
                e.dma_start(guT_d[bass.ds(c, 1)].rearrange("o p n -> (o p) n"), flat3(gus[p][:, :, :, :])).then_inc(w_stored[p], 16)
                e.dma_start(dnT_d[bass.ds(c, 1)].rearrange("o p n -> (o p) n"), flat(dns[p][:, :, :])).then_inc(w_stored[p], 16)

            def load_and_store(s, p, half):
                load_weights(s, s + RING, p)
                store_weights(s - RING, s, p)

            load_weights(0, 2, 0)
            load_weights(1, 3, 1)
            e.dma_start(iota_s[:, :], iota.broadcast_to([P, N])).then_inc(iota_in, 16)
            ring_loop(e, load_and_store, RING, NCH - RING - 1)
            for p in range(RING):
                load_weights(NCH - RING + p, p, p)
                store_weights(NCH - 2 * RING + p, NCH - RING + p, p)
            for p in range(RING):
                store_weights(NCH - RING + p, p, p)
            for n, w in enumerate((w_kv_down, w_k_up, w_v_up, w_q, w_o)):
                e.dma_start(wat[:, n, :], w).then_inc(watt_in, 16)
            e.dma_start(wrope[:, 0, :], w_k_rope).then_inc(watt_in, 16)
            e.dma_start(wrope[:, 1, :], w_q_rope).then_inc(watt_in, 16)

            def stage_weights(k, first):
                def stage(c, p, half):
                    e.wait_ge(eo_done, k * NCH + c + 1)
                    e.dma_start(flat3(gus[p][:, :, :, :]), guT_d[bass.ds(c, 1)].rearrange("o p n -> (o p) n")).then_inc(gus_in[p], 16)
                    e.dma_start(flat(dns[p][:, :, :]), dnT_d[bass.ds(c, 1)].rearrange("o p n -> (o p) n")).then_inc(dns_in[p], 16)

                ring_loop(e, stage, first, NCH - 1)

            for p in range(RING):
                e.wait_ge(w_stored[p], 16 * NCH)
            stage_weights(0, RING)

            e.wait_ge(added, NG + RING)
            e.dma_start(cs[:, 0, :], cos3).then_inc(cs_in, 16)
            e.dma_start(cs[:, 1, :], sin3).then_inc(cs_in, 16)
            e.wait_ge(rows_const, 8)
            for side, (dst, parts) in enumerate(((qn_d, "hhl"), (kn_d, "hlh"))):
                for c in range(NC):
                    u = side * NC + c
                    cols = slice(c * BANK, (c + 1) * BANK)
                    e.wait_ge(nh_ready, u + 1)
                    e.wait_ge(nl_ready, u + 1)
                    for r, part in enumerate(parts):
                        src = nh[u % RING] if part == "h" else nl[u % RING]
                        e.dma_start(dst[r, :, cols], raw(src[:, :])).then_inc(nope_stored[u % RING], 16)

            def stage_shift(pair, p, half):
                e.wait_ge(shf_ready, pair + 2)
                for h in range(2):
                    e.dma_start(raw(Qst[p][h][ROWS:ROWS + 1, :]), raw(shf[h * NT:(h + 1) * NT, :])).then_inc(shift_in[p], 16)

            def stage_pair(pair, p, part):
                for h in range(2):
                    rows = bass.ds((pair * 2 + h) * HD, HD)
                    for scratch, dst in ((kn_d, Kst), (qn_d, Qst)):
                        src = scratch[:, rows, :].rearrange("k r (b c n) -> k r b c n", b=B, n=BANK)[:, :, :, part, :]
                        to = raw(dst[p][h][ROPE3:ROWS, :]).rearrange("r (b c n) -> r b c n", b=B, n=BANK)[:, :, part, :]
                        e.dma_start(to, src).then_inc(stage_in[part][p], 16)

            def pair_step(pair, p, half):
                e.wait_ge(scores_done, pair * 2 * NS + 2 * EARLY + 2)
                stage_pair(pair + RING, p, 0)
                stage_shift(pair + 1, 1 - p, half)
                e.wait_ge(scores_done, (pair + 1) * 2 * NS)
                stage_pair(pair + RING, p, 1)

            for q in range(RING):
                e.wait_ge(nope_stored[q], 48 * NC)
            for p in range(RING):
                for part in range(2):
                    stage_pair(p, p, part)
            stage_shift(0, 0, 0)
            ring_loop(e, pair_step, 0, NPAIR - RING - 1)
            stage_shift(NPAIR - 1, 1, 0)
            stage_weights(1, 0)
            for g in range(NG):
                b, r = g * TG // TB, g * TG % TB
                e.wait_ge(added, 2 * NG + g + 1 + RING)
                e.dma_start(out[b, r * P:(r + TG) * P].rearrange("(t p) d -> p t d", p=P), x[:, g * TG:(g + 1) * TG, :]).then_inc(out_s, 16)
            e.wait_ge(out_s, 16 * NG)

        @blk.gpsimd
        def _(e):
            e.sem_inc(w_copied, 2)
            e.sem_inc(placed, RING * CE)
            for p in range(RING):
                e.sem_inc(gus_in[p], 16)
                e.sem_inc(dns_in[p], 16)
            e.sem_inc(idx_ready, 1)
            e.sem_inc(eol_ready, 1)
            e.sem_inc(bufT_ready, 1)
            e.sem_inc(silu_step, 1)
            e.sem_inc(mx_turned, 1)
            e.sem_inc(attn_ready, 2)
            e.sem_inc(shf_ready, 1)
            e.memset(onesb[:, :], 1.0).then_inc(memsets, 1)
            e.memset(zerosb[:, :], 0.0).then_inc(memsets, 1)
            e.memset(maskQw[:, 0:P], 0.0).then_inc(memsets, 1)
            e.wait_ge(consts_in, 32)
            e.tensor_copy(identb[:, :], sq[:, 0, :]).then_inc(bf_consts, 1)
            e.tensor_copy(beforeb[:, :], sq[:, 1, :]).then_inc(bf_consts, 1)
            e.tensor_copy(maskT[:, :], sq[:, 2, :]).then_inc(bf_consts, 1)
            e.tensor_copy(maskQ, sq[:, 3, :]).then_inc(bf_consts, 1)

            def split(k):
                for q in range(2):
                    e.tensor_copy(info[:, :, :, q], tokinfo_s[:, :, q:q + 1].broadcast_to([P, NT, E])).then_inc(info_const, 1)
                for g in range(NG):
                    u = k * NG + g
                    t = slice(g * TG, (g + 1) * TG)
                    e.wait_ge(rem1, u + 1)
                    e.tensor_copy(xp[:, t, 1, :], rem[g][:, :, :]).then_inc(part1, 1)
                    e.wait_ge(part1, u + 1)
                    e.tensor_tensor(xp[:, t, 2, :], rem[g][:, :, :], xp[:, t, 1, :], ALU.subtract).then_inc(split_done, 1)

            e.wait_ge(iota_in, 16)
            e.tensor_copy(iotab[:, :], iota_s[:, 0:P]).then_inc(bf_consts, 1)
            split(0)
            e.wait_ge(watt_in, 16 * 7)
            half = DR // 2
            for side in range(2):
                e.tensor_copy(wrep[:, side, 0, :, :], wrope[:, side:side + 1, :].broadcast_to([P, 3, DR])).then_inc(rope_weights, 1)
                e.tensor_copy(wrep[:, side, 1, :, 0:half], wrope[:, side:side + 1, half:DR].broadcast_to([P, 3, half])).then_inc(rope_weights, 1)
                e.tensor_copy(wrep[:, side, 1, :, half:DR], wrope[:, side:side + 1, 0:half].broadcast_to([P, 3, half])).then_inc(rope_weights, 1)
            e.wait_ge(rope_weights, 6)
            e.wait_ge(added, NG + RING)
            for p in range(RING):
                for h in range(2):
                    e.memset(raw(Kst[p][h][ROPE3:P, :]), 1.0).then_inc(rows_const, 1)
                    e.memset(raw(Qst[p][h][ROPE3:P, :]), 0.0).then_inc(rows_const, 1)
            e.wait_ge(rows_const, 8)
            for p in range(RING):
                e.memset(Vst[p][:, :, :, HD:VW], 0.0).then_inc(vst_const, 1)
            e.wait_ge(vst_const, RING)
            for p in range(RING):
                e.memset(Vst[p][:, :, :, HD:HD + 1], 1.0).then_inc(vst_const, 1)
            e.memset(mxh[:, :, :], MASKED).then_inc(mx_const, 1)

            def copy_rope(u):
                e.wait_ge(lo_ready, u + 1)
                st, cols = (Qst, Kst)[u // NC], slice(u % NC * BANK, (u % NC + 1) * BANK)
                e.tensor_copy(st[1][1][0:ROPE3, cols], st[0][0][0:ROPE3, cols]).then_inc(rope_copied, 1)

            for u in range(2 * NC):
                r = u % RING
                e.wait_ge(ra_ready, u + 1)
                e.wait_ge(rb_ready, u + 1)
                e.tensor_tensor(ra[r][:, :], ra[r][:, :], rb[r][:, :], ALU.add).then_inc(rsum_ready, 1)
                if u % 2:
                    copy_rope(u - 1)

            def stage_values(pair, p, half):
                e.wait_ge(pv_done, NS * (pair + 1))
                e.tensor_copy(Vst[p][:, :, :, 0:HD], V[:, :, bass.ds(pair * 2, 2), :]).then_inc(vst_ready, 1)

            e.wait_ge(v_ready, NG)
            ring_loop(e, stage_values, 0, NPAIR - 1)
            e.wait_ge(vst_ready, NPAIR)
            e.wait_ge(wo_done, 1)
            split(1)

        @blk.scalar
        def _(e):
            e.dma_start(sq[:, :, :], squares.rearrange("k p c -> p k c")).then_inc(consts_in, 16)
            e.dma_start(tokinfo_s[:, :, :], tokinfo).then_inc(consts_in, 16)
            e.sem_inc(xnT_ready, RING)

            def transposed(n, norm=True):
                if norm:
                    e.wait_ge(var_ready, n - n // 3 + 1)
                    e.activation(sd[:, :], var[:, :], ACT.Sqrt).then_inc(sd_ready, 1)
                for g in range(NG):
                    e.wait_ge(turned, n * NG + g + 1)
                    e.activation(xnT[:, g * BANK:(g + 1) * BANK], ps[:, g % RING, :], ACT.Copy).then_inc(xnT_ready, 1)

            def split_first(k):
                for g in range(NG):
                    t = slice(g * TG, (g + 1) * TG)
                    e.activation(xp[:, t, 0, :], xn[:, t, :], ACT.Copy).then_inc(part0, 1)

            def exps(k):
                e.wait_ge(soft, 2 + 5 * k)
                e.activation(zl[:, :, :], zl[:, :, :], ACT.Exp).then_inc(exp_done, 1)

            def experts(k):
                def gather_out(c, p):
                    e.wait_ge(gathered, k * NCH + c + 1)
                    e.wait_ge(gu_done, k * NCH + c + 1)
                    e.activation(flat(bufT[p][:, :, :]), ps[:, 0, :], ACT.Copy).then_inc(bufT_ready, 1)

                def step(c, p, h=0, last=False):
                    e.wait_ge(gu_done, k * NCH + c + 1 + RING)
                    e.wait_ge(silu_step, 2 * (k * NCH + c) + 1)
                    e.activation(flat(th[:, :, :]), ps[0:F, 1, :], ACT.Tanh, scale=0.5).then_inc(th_ready, 1)
                    if not last:
                        gather_out(c + 1, 1 - p)
                    e.wait_ge(eo_done, k * NCH + c + 1 + RING)
                    e.wait_ge(slots_ready, k * NCH + c + 1)
                    e.wait_ge(combined, CE * (k * NCH + c + 1))
                    for q in range(CE):
                        ins = e.activation(eoh[p][:, q, :], ps[:, 1, q * D:(q + 1) * D], ACT.Copy, scale=wslot[p][:, q:q + 1])
                    ins.then_inc(eoh_ready, 1)

                gather_out(0, 0)
                step(0, 0)
                ring_loop(e, step, 1, NCH - 2)
                step(NCH - 1, 1, last=True)
                e.wait_ge(y_done, k + 1)
                for j in range(NC):
                    e.activation(yT[:, j * BANK:(j + 1) * BANK], ps[:, 4 + j, :], ACT.Copy).then_inc(yT_ready, 1)

            e.wait_ge(gate_turned, 1)
            e.activation(gateT[:, :], ps[:, 2, 0:E], ACT.Copy).then_inc(gate_copied, 1)
            def copy_weights(s, p):
                e.wait_ge(gu_turned, s + 1)
                e.activation(gus[p][:, :, :, :].rearrange("p (g e) s f -> p g (e s f)", g=2), ps[:, 4:6, 0:CE * F], ACT.Copy).then_inc(w_copied, 1)
                e.wait_ge(w_turned, s + 1 + RING)
                e.activation(flat(dns[p][:, :, :]), ps[0:F, 6, :], ACT.Copy).then_inc(w_copied, 1)

            transposed(0)
            split_first(0)
            copy_weights(0, 0)
            exps(0)
            copy_weights(1, 1)
            with e.Fori(1, NCH // RING) as i:
                for p in range(RING):
                    e.wait_ge(w_stored[p], 32 * i)
                    copy_weights(i * RING + p, p)
            experts(0)
            transposed(1)

            def copy_rope(u):
                e.wait_ge(lo_ready, u + 1)
                st, cols = (Qst, Kst)[u // NC], slice(u % NC * BANK, (u % NC + 1) * BANK)
                for p, h in ((0, 1), (1, 0), (1, 1))[:2 + u % 2]:
                    e.activation(st[p][h][0:ROPE3, cols], st[0][0][0:ROPE3, cols], ACT.Copy).then_inc(rope_copied, 1)

            for u in range(2 * NC):
                r = u % RING
                side, c = u // NC, u % NC
                e.wait_ge(nope_done, u + 1)
                if u >= RING:
                    e.wait_ge(nope_stored[r], 48 * (u // RING))
                e.activation(nh[r][:, :], ps[:, 2 + r, :], ACT.Copy).then_inc(nh_ready, 1)
                if side == 0:
                    e.wait_ge(ckv_done, c + 1)
                    e.activation(ckvT[:, c * BANK:(c + 1) * BANK], ps[:, c % RING, :], ACT.Copy).then_inc(ckvT_ready, 1)
                e.wait_ge(rsum_ready, u + 1)
                dst = (Qst, Kst)[side][0][0][0:ROPE3, c * BANK:(c + 1) * BANK]
                e.activation(dst, ra[r][:, :], ACT.Copy).then_inc(hi_ready, 1)
                if u >= 1:
                    copy_rope(u - 1)
            copy_rope(2 * NC - 1)
            for g in range(NG):
                e.wait_ge(v_done, g + 1)
                e.activation(V[:, TG * g:TG * (g + 1), :, :].rearrange("p a b c -> p (a b c)"), ps[:, g % RING, :], ACT.Copy).then_inc(v_ready, 1)

            def copy_values(pair, j):
                e.wait_ge(pv_done, (pair + 2) * NS + CLOSES[j] + 1)
                e.wait_ge(o_turned, pair * 2 + j + 1)
                e.activation(oS[j][:, :], ps[:, 4 + j, :], ACT.Copy).then_inc(oS_ready, 1)

            def pair_step(pair, p, half, first=False):
                for n, (j, kt) in enumerate(STEPS):
                    lo = max(0, kt * P - j * BANK)
                    for b in range(B):
                        e.wait_ge(scores_done, pair * 2 * NS + 2 * n + b + 1)
                        if b == 0:
                            e.wait_ge(pv_done, (pair + 2) * NS + n + 1 - RING)
                        e.activation(probs[n % RING][:, 2 * b:2 * b + 2, lo:BANK], ps[:, 2 * b:2 * b + 2, lo:BANK],
                                     ACT.Exp, scale=SCALE).then_inc(probs_ready, 1)
                    if n == 0 and not first:
                        copy_values(pair - 1, 1)
                    if n == CLOSES[0] + 2:
                        copy_values(pair, 0)

            pair_step(0, 0, 0, first=True)
            ring_loop(e, pair_step, 1, NPAIR - 2)
            pair_step(NPAIR - 1, 1, 0)
            copy_values(NPAIR - 1, 1)
            transposed(2, norm=False)
            transposed(3)
            split_first(1)
            exps(1)
            experts(1)

        @blk.vector
        def _(e):
            e.sem_inc(added, RING)

            def moments_of(n, g):
                if g < NG:
                    for t in range(g * TG, (g + 1) * TG):
                        e.bn_stats(stats[:, t, :], x[:, t, :]).then_inc(stat_done, 1)
                if g >= 1:
                    e.wait_ge(stat_done, NT * n + TG * g)
                    for t in range((g - 1) * TG, g * TG):
                        e.bn_aggr(mv[:, t, :], stats[:, t, :]).then_inc(moments, 1)

            def layernorm(n):
                e.wait_ge(moments, NT * (n + 1))
                e.tensor_scalar(var[:, :], mv[:, :, 1], EPS, None, ALU.add).then_inc(var_ready, 1)
                e.wait_ge(sd_ready, n + 1)
                e.reciprocal(rstd[:, :], sd[:, :]).then_inc(rstd_ready, 1)
                e.wait_ge(rstd_ready, n + 1)
                if n >= 1:
                    e.wait_ge(split_done, NG)
                for t in range(NT):
                    e.tensor_scalar(xn[:, t, :], x[:, t, :], mv[:, t, 0:1], rstd[:, t:t + 1],
                                    ALU.subtract, ALU.mult).then_inc(xn_ready, 1)

            def split_rest(k):
                for g in range(NG):
                    t = slice(g * TG, (g + 1) * TG)
                    e.wait_ge(part0, k * NG + g + 1)
                    e.tensor_tensor(rem[g][:, :, :], xn[:, t, :], xp[:, t, 0, :], ALU.subtract).then_inc(rem1, 1)

            def route(k):
                s0 = 5 * k
                lg = ps[:, 2, :].rearrange("p (t e) -> p t e", t=NT)
                pos = ps[:, 3, :].rearrange("p (t e) -> p t e", t=NT)

                def wide_of(a):
                    return a[:, :].unsqueeze(2).broadcast_to([P, NT, E])

                e.wait_ge(logits_done, k + 1)
                e.tensor_reduce(top[:, :], lg, AX.X, ALU.max).then_inc(soft, 1)
                e.wait_ge(soft, s0 + 1)
                e.tensor_tensor(zl[:, :, :], lg, wide_of(top), ALU.subtract).then_inc(soft, 1)
                e.wait_ge(exp_done, k + 1)
                e.tensor_reduce(den[:, :], zl[:, :, :], AX.X, ALU.add).then_inc(soft, 1)
                e.wait_ge(soft, s0 + 3)
                e.reciprocal(rden[:, :], den[:, :]).then_inc(soft, 1)
                e.wait_ge(soft, s0 + 4)
                e.tensor_tensor(pr[:, :, :], zl[:, :, :], wide_of(rden), ALU.mult).then_inc(soft, 1)
                e.wait_ge(soft, s0 + 5)
                for t in range(NT):
                    e.max(t8[:, t, :], pr[:, t, :]).then_inc(top8, 1)
                e.wait_ge(top8, NT * (k + 1))
                for t in range(NT):
                    e.match_replace(rep[:, t, :], t8[:, t, :], pr[:, t, :], -1.0).then_inc(replaced, 1)
                e.wait_ge(replaced, NT * (k + 1))
                q0 = 8 * k
                e.tensor_scalar(maskb[:, :, :], rep[:, :, :], 0.0, None, ALU.is_lt).then_inc(routed, 1)
                e.tensor_reduce(den[:, :], t8[:, :, :], AX.X, ALU.add).then_inc(routed, 1)
                e.wait_ge(routed, q0 + 2)
                e.reciprocal(rden[:, :], den[:, :]).then_inc(routed, 1)
                e.tensor_tensor(wr[:, :, :], pr[:, :, :], maskb[:, :, :], ALU.mult).then_inc(routed, 1)
                e.tensor_scalar(zl[:, :, :], rep[:, :, :], 0.0, UNROUTED, ALU.is_ge, ALU.mult).then_inc(posm_ready, 1)
                e.wait_ge(routed, q0 + 4)
                e.scalar_tensor_tensor(out=pr[:, :, :], in0=wr[:, :, :], scalar=0.25, in1=wide_of(rden), op0=ALU.mult, op1=ALU.mult).then_inc(routed, 1)
                e.wait_ge(routed, q0 + 5)
                e.wait_ge(info_const, 2 * (k + 1))
                e.tensor_copy(info[:, :, :, 2], pr[:, :, :]).then_inc(routed, 1)
                e.wait_ge(routed, q0 + 6)
                e.tensor_tensor(wr[:, :, :], pr[:, :, :], info[:, :, :, 2], ALU.subtract).then_inc(routed, 1)
                e.wait_ge(routed, q0 + 7)
                e.tensor_copy(info[:, :, :, 3], wr[:, :, :]).then_inc(routed, 1)
                e.wait_ge(routed, q0 + 8)
                e.tensor_tensor(info[:, :, :, 4], wr[:, :, :], info[:, :, :, 3], ALU.subtract).then_inc(onehot_ready[k], 1)
                e.wait_ge(posm_ready, 2 * k + 1)
                e.wait_ge(pos_done, k + 1)
                e.tensor_tensor(posm[:, :, :], pos, zl[:, :, :], ALU.add).then_inc(posm_ready, 1)
                a0 = 3 * k
                e.tensor_reduce(least[:, :], pos[0:1], AX.X, ALU.min).then_inc(act_step, 1)
                e.wait_ge(act_step, a0 + 1)
                e.tensor_scalar(least[:, :], least[:, :], float(CAP), None, ALU.is_lt).then_inc(act_step, 1)
                e.wait_ge(act_step, a0 + 2)
                e.tensor_reduce(nactf[:, :], least[:, :], AX.X, ALU.add).then_inc(act_step, 1)
                e.wait_ge(act_step, a0 + 3)
                e.tensor_scalar(nact[:, :], nactf[:, :], float(LEAST), None, ALU.max).then_inc(nact_ready, 1)
                e.wait_ge(nact_ready, k + 1)
                e.wait_ge(posm_ready, 2 * k + 2)

            def experts(k):
                n = e.value_load(nact[0:1, 0:1], min_val=LEAST, max_val=NT)

                def onehots(c):
                    def tile(t):
                        for q in range(CE):
                            ins = e.tensor_scalar(onehot[:, bass.ds(t, 1), q, :].rearrange("p o c -> p (o c)"), iotab[:, :],
                                                  posm[:, bass.ds(t, 1), bass.ds(c * CE + q, 1)].rearrange("p a b -> p (a b)"),
                                                  None, ALU.is_equal)
                        ins.then_inc(onehot_ready[k], 1)

                    for t in range(LEAST - 1):
                        tile(t)
                    with e.Fori(LEAST - 1, n) as t:
                        tile(t)

                def slots(c, p):
                    u = k * NCH + c
                    e.wait_ge(gathered, u + 1)
                    e.wait_ge(placed, (u + 1) * CE)
                    e.tensor_copy(idx[:, :, 0:5], ps[:, 3, 0:CE * 8].rearrange("p (e w) -> p e w", w=8)[:, :, 0:5]).then_inc(idx_ready, 1)
                    e.wait_ge(idx_ready, u + 2)
                    e.scalar_tensor_tensor(out=tok[p][:, :], in0=idx[:, :, 1], scalar=float(P), in1=idx[:, :, 0],
                                           op0=ALU.mult, op1=ALU.add).then_inc(slot_step, 1)
                    e.tensor_tensor(wtmp[:, :], idx[:, :, 2], idx[:, :, 3], ALU.add).then_inc(slot_step, 1)
                    e.wait_ge(slot_step, 2 * u + 2)
                    e.tensor_tensor(wslot[p][:, :], wtmp[:, :], idx[:, :, 4], ALU.add).then_inc(slots_ready, 1)

                def place_slots(c, p):
                    u = k * NCH + c
                    for q in range(CE):
                        e.wait_ge(combined, (u + 1) * CE + q + 1)
                        e.tensor_scalar(place[q][:, 0:NEAR], iota_s[:, 0:NEAR], tok[p][:, q:q + 1], None, ALU.is_equal).then_inc(placed, 1)
                        with e.If(n > NEAR // P):
                            e.tensor_scalar(place[q][:, NEAR:N], iota_s[:, NEAR:N], tok[p][:, q:q + 1], None, ALU.is_equal).then_inc(placed_far[k], 1)

                def step(c, p, h=0, ahead=2, first=False):
                    u = k * NCH + c
                    e.wait_ge(th_ready, u + 1)
                    e.scalar_tensor_tensor(out=flat(ga[:, :, :]), in0=flat(th[:, :, :]), scalar=1.0, in1=ps[0:F, 1, :],
                                           op0=ALU.add, op1=ALU.mult).then_inc(silu_step, 1)
                    e.wait_ge(silu_step, 2 * u + 2)
                    e.tensor_tensor(flat(hT[:, :, :]), flat(ga[:, :, :]), ps[0:F, 2, :], ALU.mult).then_inc(silu_step, 1)
                    if not first:
                        place_slots(c - 1, 1 - p)
                    if ahead >= 1:
                        slots(c + 1, 1 - p)
                    e.wait_ge(eoh_ready, u + 1)
                    for q in range(CE):
                        ins = e.scalar_tensor_tensor(out=eol[p][:, q, :], in0=ps[:, 1, q * D:(q + 1) * D], scalar=wslot[p][:, q:q + 1],
                                                     in1=eoh[p][:, q, :], op0=ALU.mult, op1=ALU.subtract)
                    ins.then_inc(eol_ready, 1)
                    if ahead >= 2:
                        onehots(c + 2)

                onehots(0)
                slots(0, 0)
                onehots(1)
                step(0, 0, first=True)
                ring_loop(e, step, 1, NCH - 4)
                step(NCH - 3, 1)
                step(NCH - 2, 0, ahead=1)
                step(NCH - 1, 1, ahead=0)
                place_slots(NCH - 1, 1)

            def add_to_x(n):
                for g in range(NG + 1):
                    if g < NG:
                        if n == 1:
                            e.wait_ge(wo_done, g + 1)
                            bank = 2 + g % RING
                        else:
                            e.wait_ge(y_turned, (n // 2) * NG + g + 1)
                            bank = g % RING
                        t = slice(g * TG, (g + 1) * TG)
                        e.tensor_tensor(x[:, t, :], x[:, t, :], ps[:, bank, :].rearrange("p (t d) -> p t d", d=D), ALU.add).then_inc(added, 1)
                    if g >= 1 and n < 2:
                        e.wait_ge(added, NG * n + g + RING)
                        moments_of(n + 1, g - 1)
                if n < 2:
                    moments_of(n + 1, NG)

            for g in range(NG):
                e.wait_ge(x_in_s[g], 16)
                moments_of(0, g)
            moments_of(0, NG)
            layernorm(0)
            split_rest(0)
            route(0)
            e.wait_ge(bf_consts, 5)
            experts(0)
            add_to_x(0)
            layernorm(1)

            e.wait_ge(cs_in, 32)
            for u in range(2 * NC + 1):
                if u < 2 * NC:
                    side, c, r = u // NC, u % NC, u % RING
                    cols = slice(c % (T // BANK) * BANK, (c % (T // BANK) + 1) * BANK)
                    e.wait_ge(rope_done, u + 1)
                    if u >= RING:
                        e.wait_ge(lo_ready, u - RING + 1)
                    e.tensor_tensor(ra[r][:, :], ps[0:ROPE3, 4 + 2 * r, :], cs[:, 0, cols], ALU.mult).then_inc(ra_ready, 1)
                    e.tensor_tensor(rb[r][:, :], ps[0:ROPE3, 5 + 2 * r, :], cs[:, 1, cols], ALU.mult).then_inc(rb_ready, 1)
                    e.wait_ge(nh_ready, u + 1)
                    e.tensor_tensor(nl[r][:, :], ps[:, 2 + r, :], nh[r][:, :], ALU.subtract).then_inc(nl_ready, 1)
                if u >= 1:
                    v = u - 1
                    side, c, r = v // NC, v % NC, v % RING
                    dst = (Qst, Kst)[side][0][0][:, c * BANK:(c + 1) * BANK]
                    low = (slice(2 * DR, 3 * DR), slice(DR, 2 * DR))[side]
                    e.wait_ge(hi_ready, v + 1)
                    e.tensor_tensor(dst[low], ra[r][low, :], dst[low], ALU.subtract).then_inc(lo_ready, 1)

            def maxima(pair, first, last, banks=RING):
                for m in range(first, last):
                    jt, o, w, q, nq = UNITS[m]
                    e.wait_ge(mscores_done, pair * NU + m + 1)
                    e.tensor_reduce(mxh[:, o // BANK, :].rearrange("p (q t) -> p q t", t=TB)[:, q:q + nq, jt],
                                    ps[:, 7 - m % banks, 0:nq * w].rearrange("p (q k) -> p q k", k=w), AX.X, ALU.max).then_inc(mx_ready, 1)

            def shifts(pair):
                e.wait_ge(mx_ready, (pair + 1) * NU + RING)
                e.tensor_tensor(mx[:, :], mxh[:, 0, :], mxh[:, 1, :], ALU.max).then_inc(mx_joined, 1)
                e.wait_ge(mx_turned, pair + 2)
                e.tensor_scalar(shf[:, :], ps[0:2 * NT, 7, 0:P], -1.0, None, ALU.mult).then_inc(shf_ready, 1)

            def normalise(pair, j):
                u = pair * 2 + j
                e.wait_ge(o_turned, u + 3)
                o = ps[:, 4 + j, :].rearrange("p (t s c) -> p t s c", t=4, s=4)
                e.wait_ge(attn_ready, u + 2)
                e.reciprocal(ord_[:, :, :], o[:, :, :, HD]).then_inc(oden_ready, 1)
                e.wait_ge(oden_ready, u + 1)
                for b in range(B):
                    dst = attn[:, b * TB + 4 * j:b * TB + 4 * j + 4, bass.ds(pair * 2 * HD, 2 * HD)].rearrange("p t (h c) -> p t h c", h=2)
                    ins = e.tensor_tensor(dst, o[:, :, 2 * b:2 * b + 2, 0:HD],
                                          ord_[:, :, 2 * b:2 * b + 2].unsqueeze(3).broadcast_to([P, 4, 2, HD]), ALU.mult)
                ins.then_inc(attn_ready, 1)

            def pair_step(pair, p=0, h=0, first=False, last=False):
                if not last:
                    maxima(pair + 1, 0, BEFORE[1])
                if not first:
                    normalise(pair - 1, 1)
                if last:
                    normalise(pair, 0)
                else:
                    turned_at = BEFORE[CLOSES[0] + 3]
                    maxima(pair + 1, BEFORE[1], turned_at)
                    normalise(pair, 0)
                    maxima(pair + 1, turned_at, NU)
                    e.wait_ge(shift_in[p], 32 * (h + 1))
                    shifts(pair + 1)

            e.wait_ge(mx_const, 1)
            maxima(0, 0, NU, banks=4)
            shifts(0)
            pair_step(0, first=True)
            ring_loop(e, pair_step, 1, NPAIR - 2)
            pair_step(NPAIR - 1, last=True)
            normalise(NPAIR - 1, 1)
            add_to_x(1)
            layernorm(2)
            split_rest(1)
            route(1)
            experts(1)
            add_to_x(2)

        @blk.tensor
        def _(e):
            e.sem_inc(w_turned, RING)
            e.sem_inc(gu_done, RING)
            e.sem_inc(eo_done, RING)
            e.sem_inc(combined, 2 * CE)
            e.sem_inc(mx_ready, RING)
            e.sem_inc(probs_ready, RING)
            e.sem_inc(pv_done, 2 * NS)
            e.sem_inc(oS_ready, 2)
            e.sem_inc(o_turned, 2)

            def transposes(n, src):
                for g in range(NG):
                    if n != 2:
                        e.wait_ge(xn_ready, (n - n // 3) * NT + (g + 1) * TG)
                    e.wait_ge(xnT_ready, n * NG + g + 1)
                    for q in range(TG):
                        ins = e.transpose(ps[:, g % RING, q * P:(q + 1) * P], src[:, g * TG + q, :], ident)
                    ins.then_inc(turned, 1)

            def logits(k):
                for t in range(NT):
                    if t % TG == 0:
                        e.wait_ge(xnT_ready, 3 * k * NG + t // TG + 1 + RING)
                    ins = e.matmul(ps[:, 2, t * E:(t + 1) * E], xnT[:, t * P:(t + 1) * P], gateT[:, :], start=True, stop=True)
                ins.then_inc(logits_done, 1)

            def turn_weights(s, p, half):
                e.wait_ge(nat_in[p], 32 * (half + 1))
                e.wait_ge(w_copied, 2 * s + 1)
                for q in range(2 * CE):
                    ins = e.transpose(ps[:, 4 + q // CE, (q % CE) * F:(q % CE + 1) * F], wgn[p][:, q, :], ident[0:F, 0:F])
                ins.then_inc(gu_turned, 1)
                e.wait_ge(w_copied, 2 * s + 2)
                for q in range(CE):
                    ins = e.transpose(ps[0:F, 6, q * D:(q + 1) * D], wdn[p][:, q, :], ident)
                ins.then_inc(w_turned, 1)

            def positions(k):
                e.wait_ge(routed, 8 * k + 1)
                e.matmul(ps[:, 3, :], zerosb[:, 0:P], zerosb[:, :], start=True, stop=False, skip_group_check=True)
                for t in range(NT - 1):
                    o = ps[:, 3, (t + 1) * E:].rearrange("p (t e) -> p t e", e=E)
                    e.matmul(o, onesb[:, :], maskb[:, t:t + 1, :].broadcast_to([P, NT - 1 - t, E]),
                             start=False, stop=False, skip_group_check=True)
                e.matmul(ps[:, 3, :], beforeb[:, :], flat(maskb[:, :, :]), start=False, stop=True, skip_group_check=True).then_inc(pos_done, 1)

            def experts(k):
                def open_sums():
                    for j in range(NC):
                        e.matmul(ps[:, 4 + j, :], zerosb[:, 0:P], zerosb[:, :], start=True, stop=False, skip_group_check=True)

                if k == 1:
                    open_sums()
                e.wait_ge(nact_ready, k + 1)
                n = e.value_load(nact[0:1, 0:1], min_val=LEAST, max_val=NT)
                e.wait_ge(split_done, NG * (k + 1))

                def gather(c, p):
                    u = k * NCH + c
                    e.wait_ge(bufT_ready, u + 1)
                    e.wait_ge(idx_ready, u + 1)

                    def tile(t, first=False, last=False):
                        e.wait_ge(onehot_ready[k], c * n + t + 2)
                        for part in range(3):
                            e.matmul(ps[:, 0, :], xp[:, bass.ds(t, 1), part, :].rearrange("p o d -> p (o d)"),
                                     onehot[:, bass.ds(t, 1), :, :].rearrange("p o e c -> p (o e c)"),
                                     start=first and part == 0, stop=last and part == 2, skip_group_check=True)
                        for q in range(CE):
                            ins = e.matmul(ps[:, 3, q * 8:q * 8 + 5], onehot[:, bass.ds(t, 1), q, :].rearrange("p o c -> p (o c)"),
                                           info[:, bass.ds(t, 1), bass.ds(c * CE + q, 1), :].rearrange("p a b w -> p (a b w)"),
                                           start=first and q == 0, stop=last, skip_group_check=True)
                        if last:
                            ins.then_inc(gathered, 1)

                    tile(0, first=True)
                    for t in range(1, LEAST - 2):
                        tile(t)
                    with e.Fori(LEAST - 2, n - 1) as t:
                        tile(t)
                    tile(n - 1, last=True)

                def combine(c, p):
                    u = k * NCH + c
                    e.wait_ge(eoh_ready, u + 1)
                    e.wait_ge(eol_ready, u + 2)
                    for q in range(CE):
                        e.wait_ge(placed, (u + RING) * CE + q + 1)
                        with e.If(n > NEAR // P):
                            e.wait_ge(placed_far[k], c * CE + q + 1)
                            for w in (eoh, eol):
                                for o, m in ((NEAR, 256), (2 * BANK, BANK), (3 * BANK, BANK)):
                                    e.matmul(ps[:, 4 + o // BANK, o % BANK:o % BANK + m], w[p][:, q, :], place[q][:, o:o + m],
                                             start=False, stop=False, skip_group_check=True)
                        for w in (eoh, eol):
                            for o, m in ((0, BANK), (BANK, 256)):
                                ins = e.matmul(ps[:, 4 + o // BANK, 0:m], w[p][:, q, :], place[q][:, o:o + m],
                                               start=False, stop=False, skip_group_check=True)
                        ins.then_inc(combined, 1)

                def step(c, p, h, first=False, last=False):
                    u = k * NCH + c
                    e.wait_ge(bufT_ready, u + 2)
                    e.wait_ge(gus_in[p], 16 * (k * NCH // RING + h + 1))
                    e.wait_ge(eol_ready, u + 1)
                    for half, bank in ((0, 1), (1, 2)):
                        for q in range(CE):
                            ins = e.matmul(ps[0:F, bank, q * CAP:(q + 1) * CAP], gus[p][:, q, half, :], bufT[p][:, q, :], start=True, stop=True)
                    ins.then_inc(gu_done, 1)
                    if not last:
                        gather(c + 1, 1 - p)
                    e.wait_ge(silu_step, 2 * u + 3)
                    e.wait_ge(dns_in[p], 16 * (k * NCH // RING + h + 1))
                    for q in range(CE):
                        ins = e.matmul(ps[:, 1, q * D:(q + 1) * D], hT[:, q, :], dns[p][:, q, :], start=True, stop=True)
                    ins.then_inc(eo_done, 1)
                    if not first:
                        combine(c - 1, 1 - p)

                gather(0, 0)
                if k == 0:
                    ring_loop(e, turn_weights, 6, 7)
                    e.wait_ge(w_copied, 2 * NCH + 2)
                    open_sums()
                step(0, 0, 0, first=True)
                ring_loop(e, step, 1, NCH - 2)
                step(NCH - 1, 1, (NCH - 1) // RING, last=True)
                combine(NCH - 1, 1)
                for j in range(NC):
                    ins = e.matmul(ps[:, 4 + j, :], zerosb[:, 0:P], zerosb[:, :], start=False, stop=True, skip_group_check=True)
                ins.then_inc(y_done, 1)
                for g in range(NG):
                    e.wait_ge(yT_ready, k * NC + g + 1)
                    e.wait_ge(added, 2 * k * NG + g + 1)
                    for q in range(TG):
                        t = g * TG + q
                        ins = e.transpose(ps[:, g % RING, q * D:(q + 1) * D], yT[:, t * P:(t + 1) * P], ident)
                    ins.then_inc(y_turned, 1)

            e.wait_ge(consts_in, 32)
            e.wait_ge(gate_in, 16)
            e.transpose(ps[:, 2, 0:E], gate_n[:, :], ident[0:E, 0:E]).then_inc(gate_turned, 1)
            e.wait_ge(bf_consts, 4)
            e.wait_ge(memsets, 3)
            e.wait_ge(gate_copied, 1)
            transposes(0, xn)
            turn_weights(0, 0, 0)
            logits(0)
            turn_weights(1, 1, 0)
            ring_loop(e, turn_weights, 2, 3)
            positions(0)
            ring_loop(e, turn_weights, 4, 5)
            experts(0)
            transposes(1, xn)

            e.wait_ge(watt_in, 16 * 7)
            e.wait_ge(rope_weights, 6)
            for u in range(2 * NC):
                side, c, r = u // NC, u % NC, u % RING
                src, w = ((xnT, 3), (ckvT, 1))[side]
                cols = slice(c * BANK, (c + 1) * BANK)
                if side == 0:
                    e.wait_ge(xnT_ready, NG + c + 1 + RING)
                else:
                    e.wait_ge(ckvT_ready, c + 1)
                if u >= RING:
                    e.wait_ge(nl_ready, u - 1)
                    e.wait_ge(rb_ready, u - 1)
                e.matmul(ps[:, 2 + r, :], wat[:, w, :], src[:, cols], start=True, stop=True).then_inc(nope_done, 1)
                if side == 0:
                    if c >= RING:
                        e.wait_ge(ckvT_ready, c - 1)
                    else:
                        e.wait_ge(xnT_ready, 2 * NG + RING)
                    e.matmul(ps[:, c % RING, :], wat[:, 0, :], xnT[:, cols], start=True, stop=True).then_inc(ckv_done, 1)
                for v in range(2):
                    ins = e.matmul(ps[0:ROPE3, 4 + 2 * r + v, :], wrep[:, 1 - side, v, :, :].rearrange("p r d -> p (r d)"), src[:, cols], start=True, stop=True)
                ins.then_inc(rope_done, 1)
            e.wait_ge(ckvT_ready, NC)
            for g in range(NG):
                if g >= RING:
                    e.wait_ge(v_ready, g - 1)
                for q in range(TG):
                    t = TG * g + q
                    ins = e.matmul(ps[:, g % RING, q * P:(q + 1) * P], ckvT[:, t * P:(t + 1) * P], wat[:, 2, :], start=True, stop=True)
                ins.then_inc(v_done, 1)

            e.wait_ge(rope_copied, 6 * NC)
            e.wait_ge(lo_ready, 2 * NC)
            e.wait_ge(nl_ready, 2 * NC)
            e.wait_ge(v_ready, NG)

            def maxima(pair, p, half, first, last, banks=RING):
                for m in range(first, last):
                    jt, o, w, q0, nq = UNITS[m]
                    if m == EARLYU:
                        e.wait_ge(stage_in[1][p], 64 * (half + 1))
                    bank = 7 - m % banks
                    diagonal = o + w == (jt + 1) * P
                    if banks == RING:
                        e.wait_ge(mx_ready, pair * NU + m + 1)
                    elif m >= banks:
                        e.wait_ge(mx_ready, m + 1 - banks + RING)
                    covered = nq > 1
                    if covered:
                        e.matmul(ps[:, bank, :].rearrange("p (q k) -> p q k", k=w), identb[:, :],
                                 maskQw[:, 2 * P - w:2 * P].unsqueeze(1).broadcast_to([P, nq, w]), start=True, stop=False, skip_group_check=True)
                    for i in range(nq):
                        h, b = (q0 + i) // B, (q0 + i) % B
                        ins = e.matmul(ps[:, bank, i * w:(i + 1) * w], Qst[p][h][0:ROWS, b * T + jt * P:b * T + (jt + 1) * P],
                                       Kst[p][h][0:ROWS, b * T + o:b * T + o + w], start=not covered,
                                       stop=covered or not diagonal, skip_group_check=True)
                        if diagonal and not covered:
                            ins = e.matmul(ps[:, bank, (i + 1) * w - P:(i + 1) * w], identb[:, :], maskQ,
                                           start=False, stop=True, skip_group_check=True)
                    ins.then_inc(mscores_done, 1)

            def turn_maxima(pair):
                e.wait_ge(mx_joined, pair + 1)
                e.transpose(ps[0:2 * NT, 7, 0:P], mx[:, :], ident).then_inc(mx_turned, 1)

            e.wait_ge(rb_ready, 2 * NC)
            e.wait_ge(stage_in[0][0], 64)
            maxima(0, 0, 0, 0, NU, banks=4)
            turn_maxima(0)

            e.wait_ge(vst_const, 2 * RING)

            def turn(pair, j):
                u = pair * 2 + j
                e.wait_ge(oS_ready, u + 1 + 2)
                for q in range(4):
                    ins = e.transpose(ps[:, 4 + j, q * P:(q + 1) * P], oS[j][:, q * P:(q + 1) * P], ident)
                ins.then_inc(o_turned, 1)

            def scores(pair, p, n, unit=None):
                j, kt = STEPS[n]
                lo = max(0, kt * P - j * BANK)
                diagonal = kt * P >= j * BANK
                for b in range(B):
                    e.wait_ge(probs_ready, pair * 2 * NS + 2 * n + b + 1)
                    for h in range(2):
                        ins = e.matmul(ps[:, 2 * b + h, lo:BANK], Kst[p][h][0:ROWS + 1, b * T + kt * P:b * T + (kt + 1) * P],
                                       Qst[p][h][0:ROWS + 1, b * T + j * BANK + lo:b * T + (j + 1) * BANK],
                                       start=True, stop=not diagonal, skip_group_check=True)
                        if diagonal:
                            ins = e.matmul(ps[:, 2 * b + h, lo:lo + P], identb[:, :], maskT[:, :], start=False, stop=True, skip_group_check=True)
                        if h == 1:
                            ins.then_inc(scores_done, 1)
                        if unit:
                            unit(n - 1, 2 * b + h, 8)

            def pair_step(pair, p, half, first=False, last=False):
                e.wait_ge(vst_ready, pair + 1)

                def unit(n, k, of):
                    if not last:
                        maxima(pair + 1, 1 - p, half + p, BEFORE[n] + SHARE[n] * k // of, BEFORE[n] + SHARE[n] * (k + 1) // of)

                def weighted(n):
                    j, kt = STEPS[n]
                    lo = max(0, kt * P - j * BANK)
                    e.wait_ge(probs_ready, pair * 2 * NS + 2 * n + 2 + RING)
                    if n == OPENS[j]:
                        e.wait_ge(attn_ready, pair * 2 + j + 1)
                    for q in range(4):
                        b, h = q // 2, q % 2
                        ins = e.matmul(ps[VW * q:VW * (q + 1), 4 + j, lo:BANK], Vst[p][:, b * TB + kt, h, :], probs[n % RING][:, q, lo:BANK],
                                       start=(n == OPENS[j]), stop=(n == CLOSES[j]), skip_group_check=True)
                        if q == 3:
                            ins.then_inc(pv_done, 1)
                        unit(n, 4 + q, 8)

                for n in range(NS):
                    if n == 1 and not first:
                        turn(pair - 1, 1)
                    if n == FIRSTU and not last:
                        e.wait_ge(stage_in[0][1 - p], 64 * (half + p + 1))
                        e.wait_ge(shf_ready, pair + 2)
                    if n == CLOSES[0] + 3:
                        turn(pair, 0)
                    if n + 1 < NS:
                        scores(pair, p, n + 1, unit)
                    elif not last:
                        e.wait_ge(shift_in[1 - p], 32 * (half + p + 1))
                        scores(pair + 1, 1 - p, 0)
                    if n == LASTU + 1 and not last:
                        turn_maxima(pair + 1)
                    weighted(n)

            e.wait_ge(shift_in[0], 32)
            scores(0, 0, 0)
            pair_step(0, 0, 0, first=True)
            ring_loop(e, pair_step, 1, NPAIR - 2)
            pair_step(NPAIR - 1, 1, (NPAIR - 1) // RING, last=True)
            turn(NPAIR - 1, 1)

            e.wait_ge(attn_ready, 2 * NPAIR + 2)
            transposes(2, attn)
            for g in range(NG):
                e.wait_ge(xnT_ready, 2 * NG + g + 1 + RING)
                e.wait_ge(added, NG + g + 1)
                for q in range(TG):
                    t = g * TG + q
                    ins = e.matmul(ps[:, 2 + g % RING, q * D:(q + 1) * D], xnT[:, t * P:(t + 1) * P], wat[:, 4, :], start=True, stop=True)
                ins.then_inc(wo_done, 1)
            transposes(3, xn)
            logits(1)
            positions(1)
            experts(1)


_INS = ['L0_attn_x', 'L0_attn_W_kv_down', 'L0_attn_W_k_up', 'L0_attn_W_v_up', 'L0_attn_W_q', 'L0_attn_W_q_rope',
        'L0_attn_W_k_rope', 'L0_attn_W_o', 'L0_ffn_gate_weight', 'L0_ffn_gate_up_proj', 'L0_ffn_down_proj']


def constants():
    a = np.arange(P)
    before = (a[:, None] < a[None, :]).astype(np.float32)
    masked = np.float32(MASKED)
    squares = np.stack([np.eye(P, dtype=np.float32), before, masked * before.T, masked * before])
    inv_freq = np.float32(1.0) / np.power(np.float32(10000.0), np.arange(0, DR, 2, dtype=np.float32) / np.float32(DR))
    angle = (np.arange(T, dtype=np.float32)[None, :] * inv_freq.astype(np.float32)[:, None]).astype(np.float32)
    c, s = np.cos(angle), np.sin(angle)
    return {
        "squares": squares.astype(np.float32),
        "cos3": np.tile(np.concatenate([c, c]), (3, 1)).astype(np.float32),
        "sin3": np.tile(np.concatenate([-s, s]), (3, 1)).astype(np.float32),
        "iota": np.arange(N, dtype=np.float32)[None, :],
        "tokinfo": np.stack(np.broadcast_arrays(a[:, None], np.arange(NT)[None, :]), -1).astype(np.float32),
    }


def kernel(**inputs):
    from concourse import bacc
    from concourse.bass_utils import run_bass_kernel_spmd

    nc = bacc.Bacc("TRN2", target_bir_lowering=False, num_devices=1)
    arrays, args = {}, []
    given = {n: np.ascontiguousarray(inputs[n]) for n in _INS}
    for name, a in {**given, **constants()}.items():
        arrays[f"in_{name}"] = a
        args.append(nc.dram_tensor(f"in_{name}", a.shape, mybir.dt.from_np(a.dtype), kind="ExternalInput").ap())
    args.append(nc.dram_tensor("out_0", (B, T, D), F32, kind="ExternalOutput").ap())
    build(nc, *args)
    r = run_bass_kernel_spmd(nc, [arrays], core_ids=[0])
    return r.results[0]["out_0"]
```
